# Optimizing a Trainium2 kernel written in Bass

```python
import numpy as np
import jax
import jax.numpy as jnp

def _softmax(x, axis=-1):
    return jax.nn.softmax(x, axis=axis)

def _gelu(x):
    return jax.nn.gelu(x, approximate=True)

def _silu(x):
    return jax.nn.silu(x)

def _sigmoid(x):
    return jax.nn.sigmoid(x)

def _layernorm(x, axis=-1, eps=1e-05):
    m = jnp.mean(x, axis=axis, keepdims=True)
    v = jnp.var(x, axis=axis, keepdims=True)
    return (x - m) / jnp.sqrt(v + eps)

def _scatter_add(tgt, idx, src, axis=0):
    return tgt.at[idx].add(src)

def _segment_sum(src, seg, n):
    return jax.ops.segment_sum(src, seg, n)
kernel_name = 'mk_gnn_ffn_d1_gnn_r8_130099'

def setup_inputs(seed: int=0):
    np.random.seed(seed)
    _w = jnp.asarray

    def _rec_inputs():
        import jax
        import jax.numpy as jnp
        _gk = jax.random.key(seed)
        x = -0.0006008 + 1.001 * jax.random.normal(jax.random.fold_in(_gk, 1), (6250, 256), jnp.float32)
        _s = jax.random.randint(jax.random.fold_in(_gk, 2), (50000,), 0, 6250, jnp.int32)
        _d = jax.random.randint(jax.random.fold_in(_gk, 3), (50000,), 0, 6250, jnp.int32)
        _loop = jnp.arange(6250, dtype=jnp.int32)
        src = jnp.concatenate([_s, _d, _loop])
        dst = jnp.concatenate([_d, _s, _loop])
        _o = jnp.argsort(dst, stable=True)
        src = src[_o]
        dst = dst[_o]
        return (x, src, dst)
    x, src, dst = _rec_inputs()

    def _L0_gnn_setup():
        import jax, jax.numpy as jnp
        import numpy as np
        N_NODES = 1250
        N_EDGES = 20000
        D = 256
        P = 2.0
        key = jax.random.key(seed)
        k1, k2, k3, k4 = jax.random.split(key, 4)
        X = jax.random.normal(k1, (N_NODES, D), dtype=jnp.float32)
        edge_index = jax.random.randint(k2, (2, N_EDGES), 0, N_NODES, dtype=jnp.int64)
        scale = 1.0 / np.sqrt(D)
        W_root = jax.random.normal(k3, (D, D), dtype=jnp.float32) * scale
        W_neigh = jax.random.normal(k4, (D, D), dtype=jnp.float32) * scale
        b = jnp.zeros((D,), dtype=jnp.float32)
        return {'X': X, 'edge_index': edge_index, 'W_root': W_root, 'W_neigh': W_neigh, 'b': b}
    _L0_gnn_all = _L0_gnn_setup()
    _L0_gnn_in = {k: v for k, v in _L0_gnn_all.items() if k in ('W_root', 'W_neigh', 'b')}
    del _L0_gnn_all

    def _L0_ffn_setup():
        import jax, jax.numpy as jnp
        import numpy as np
        E, D, H, TOP_K = (6, 256, 256, 2)
        ROUTER_H = D // 2
        key = jax.random.key(seed)
        ks = jax.random.split(key, 12)
        s = 1.0 / np.sqrt(D)
        sh = 1.0 / np.sqrt(H)
        sr = 1.0 / np.sqrt(ROUTER_H)
        return {'features': jax.random.normal(ks[0], (8, 512, D), dtype=jnp.float32), 'router_w1': jax.random.uniform(ks[1], (D, ROUTER_H), jnp.float32, -s, s), 'router_b1': jnp.zeros((ROUTER_H,), jnp.float32), 'router_w2': jax.random.uniform(ks[2], (ROUTER_H, E), jnp.float32, -sr, sr), 'router_b2': jnp.zeros((E,), jnp.float32), 'expert_w1': jax.random.uniform(ks[3], (E, D, H), jnp.float32, -s, s), 'expert_b1': jnp.zeros((E, H), jnp.float32), 'expert_w2': jax.random.uniform(ks[4], (E, H, H), jnp.float32, -sh, sh), 'expert_b2': jnp.zeros((E, H), jnp.float32), 'expert_w3': jax.random.uniform(ks[5], (E, H, D), jnp.float32, -sh, sh), 'expert_b3': jnp.zeros((E, D), jnp.float32)}
    _L0_ffn_all = _L0_ffn_setup()
    _L0_ffn_in = {k: v for k, v in _L0_ffn_all.items() if k in ('router_w1', 'router_b1', 'router_w2', 'router_b2', 'expert_w1', 'expert_b1', 'expert_w2', 'expert_b2', 'expert_w3', 'expert_b3')}
    del _L0_ffn_all
    return {'x': x, 'src': src, 'dst': dst, 'L0_gnn_W_root': _L0_gnn_in['W_root'], 'L0_gnn_W_neigh': _L0_gnn_in['W_neigh'], 'L0_gnn_b': _L0_gnn_in['b'], 'L0_ffn_router_w1': _L0_ffn_in['router_w1'], 'L0_ffn_router_b1': _L0_ffn_in['router_b1'], 'L0_ffn_router_w2': _L0_ffn_in['router_w2'], 'L0_ffn_router_b2': _L0_ffn_in['router_b2'], 'L0_ffn_expert_w1': _L0_ffn_in['expert_w1'], 'L0_ffn_expert_b1': _L0_ffn_in['expert_b1'], 'L0_ffn_expert_w2': _L0_ffn_in['expert_w2'], 'L0_ffn_expert_b2': _L0_ffn_in['expert_b2'], 'L0_ffn_expert_w3': _L0_ffn_in['expert_w3'], 'L0_ffn_expert_b3': _L0_ffn_in['expert_b3']}

def reference(x, src, dst, L0_gnn_W_root, L0_gnn_W_neigh, L0_gnn_b, L0_ffn_router_w1, L0_ffn_router_b1, L0_ffn_router_w2, L0_ffn_router_b2, L0_ffn_expert_w1, L0_ffn_expert_b1, L0_ffn_expert_w2, L0_ffn_expert_b2, L0_ffn_expert_w3, L0_ffn_expert_b3):
    import jax
    import jax.numpy as jnp

    def _L0_gnn_ref(X, edge_index, W_root, W_neigh, b):
        import jax, jax.numpy as jnp
        import numpy as np
        N_NODES = 1250
        N_EDGES = 20000
        D = 256
        P = 2.0
        n = X.shape[0]
        row, col = (edge_index[0], edge_index[1])
        ones = jnp.ones((row.shape[0],), dtype=X.dtype)
        deg = jax.ops.segment_sum(ones, row, num_segments=n)
        denom = jnp.maximum(deg, 1.0)[:, None]
        neigh_sum = jax.ops.segment_sum(X[col], row, num_segments=n)
        neigh_mean = neigh_sum / denom
        H = jax.nn.relu(X @ W_root + neigh_mean @ W_neigh + b)
        diffs = jnp.abs(H[row] - H[col]) ** P
        gg = jax.ops.segment_sum(diffs, row, num_segments=n) / denom
        return jnp.tanh(gg)

    def _L0_ffn_ref(features, router_w1, router_b1, router_w2, router_b2, expert_w1, expert_b1, expert_w2, expert_b2, expert_w3, expert_b3):
        import jax, jax.numpy as jnp
        import numpy as np
        E, D, H, TOP_K = (6, 256, 256, 2)
        ROUTER_H = D // 2
        rh = jax.nn.relu(features @ router_w1 + router_b1)
        expert_logits = jax.nn.softmax(rh @ router_w2 + router_b2, axis=-1)
        top_w, top_i = jax.lax.top_k(expert_logits, TOP_K)
        routing_weights = jax.nn.softmax(top_w, axis=-1)
        h1 = jax.nn.relu(jnp.einsum('bsd,edh->bseh', features, expert_w1) + expert_b1)
        h2 = jax.nn.relu(jnp.einsum('bseh,ehf->bsef', h1, expert_w2) + expert_b2)
        expert_out = jnp.einsum('bsef,efo->bseo', h2, expert_w3) + expert_b3
        sel = jnp.take_along_axis(expert_out, top_i[:, :, :, None], axis=2)
        combined = jnp.sum(sel * routing_weights[..., None], axis=2)
        return combined
    edge_index = jnp.stack([src, dst])
    x = x + _L0_gnn_ref(_layernorm(x, axis=-1), edge_index, L0_gnn_W_root, L0_gnn_W_neigh, L0_gnn_b)
    x = x + _L0_ffn_ref(_layernorm(x, axis=-1)[None], L0_ffn_router_w1, L0_ffn_router_b1, L0_ffn_router_w2, L0_ffn_router_b2, L0_ffn_expert_w1, L0_ffn_expert_b1, L0_ffn_expert_w2, L0_ffn_expert_b2, L0_ffn_expert_w3, L0_ffn_expert_b3)[0]
    return x

_drawn_inputs = setup_inputs


def setup_inputs(seed=0):
    import zlib

    import numpy as np

    out = dict(_drawn_inputs(seed))
    spreads = {'L0_gnn_b': (0.0, 0.1),
     'L0_ffn_router_b1': (0.0, 0.1),
     'L0_ffn_router_b2': (0.0, 0.1),
     'L0_ffn_expert_b1': (0.0, 0.767),
     'L0_ffn_expert_b2': (0.0, 0.325),
     'L0_ffn_expert_b3': (0.0, 0.1)}
    factors = {}
    for name, (base, spread) in spreads.items():
        noise = np.random.default_rng([zlib.crc32(name.encode()), seed]).standard_normal(out[name].shape)
        drawn = base * np.exp(spread * noise) if base else spread * noise
        out[name] = jnp.asarray(drawn.astype(out[name].dtype))
    for name, factor in factors.items():
        out[name] = (out[name] * factor).astype(out[name].dtype)
    return out
```

```python
from contextlib import ExitStack

import concourse.bass as bass
from concourse import mybir

F32 = mybir.dt.float32
F16 = mybir.dt.float16
I32 = mybir.dt.int32
U32 = mybir.dt.uint32
ALU = mybir.AluOpType
ACT = mybir.ActivationFunctionType
AX_X = mybir.AxisListType.X

P = 128
EPS = 1e-5
RING = 6
BANKS = 4
LAG = 2
TOP_PAD = 8
GROUP = 4


class Lane:

    def __init__(self, sem):
        self.sem, self.value = sem, 0

    def add(self, by):
        self.value += by
        return (self, self.value)


class Queue:

    def __init__(self, lane):
        self.steps, self.lane, self.seen = [], lane, {}

    def put(self, issue, after=(), lane=None, by=1):
        waits = []
        for other, value in after:
            if self.seen.get(id(other), 0) < value:
                self.seen[id(other)] = value
                waits.append((other.sem, value))
        lane = lane or self.lane
        self.steps.append((waits, issue, lane.sem, by))
        return lane.add(by)

    def dma(self, lane, out, in_, after=()):
        return self.put(lambda e: e.dma_start(out, in_), after, lane, 16)

    def wait(self, event):
        self.steps.append(([(event[0].sem, event[1])], None, None, 0))

    def run(self, engine):
        for waits, issue, sem, by in self.steps:
            for other, value in waits:
                engine.wait_ge(other, value)
            if issue is not None:
                issue(engine).then_inc(sem, by)


def gnn_moe_kernel(nc, x, src, dst, w_root, w_neigh, b_gnn, rw1, rb1, rw2, rb2,
                   ew1, eb1, ew2, eb2, ew3, eb3, out):
    N, D = x.shape
    E = src.shape[0]
    NE, _, HID = ew1.shape
    RH = rw1.shape[1]
    KD = D // P
    KH = HID // P
    NB = -(-N // P)
    LAST = N - (NB - 1) * P
    FULL, TAIL = divmod(E, P)
    T = FULL + (TAIL > 0)
    NT = (E + NB * (P - 1)) // P
    TJ = -(-NT // P)
    W1 = D + 2
    W2 = 2 * D
    CODE = 256

    with ExitStack() as ctx:
        def sb(name, shape, dt=F32):
            return ctx.enter_context(nc.sbuf_tensor(name, shape, dt))

        def lane(name):
            return Lane(ctx.enter_context(nc.semaphore(name)))

        xn_table = nc.dram_tensor("xn_table", [NB * P, D], F32, kind="Internal").ap()
        h_table = nc.dram_tensor("h_table", [NB * P, D], F32, kind="Internal").ap()
        edge_list = nc.dram_tensor("edge_list", [P * NT, 1], F32, kind="Internal").ap()
        block_of = nc.dram_tensor("block_of", [1, P * TJ], I32, kind="Internal").ap()

        node = sb("node", [P, NB, D])
        big = sb("big", [P, NB * W2])
        rank = big[:, 0:NB * T // 2 + 1].bitcast(F16)[:, 0:NB * T].rearrange("p (b t) -> p b t", b=NB)
        acc = big[:, :]
        xnT = big[:, 0:NB * D].rearrange("p (b k m) -> p b k m", b=NB, k=KD)
        spare = big[:, NB * D:]
        edges = sb("edges", [P, 4 * T])
        src_i = edges[:, 0:T].bitcast(I32)
        dst_i = edges[:, T:2 * T].bitcast(I32)
        code = edges[:, 2 * T:3 * T]
        place = edges[:, 3 * T:4 * T]
        scratch = big[:, NB * T // 2 + 1:]
        bucket_i = scratch[:, 0:T].bitcast(I32)
        bucket_h = scratch[:, T:2 * T].bitcast(F16)[:, 0:T]
        hot_h = [scratch[:, (2 + i) * T:(3 + i) * T].bitcast(F16)[:, 0:T] for i in range(2)]
        term = scratch[:, 4 * T:5 * T]
        work = sb("work", [P, RING * W2])
        rows = work[:, :].rearrange("p (r w) -> p r w", r=RING)
        hot = sb("hot", [P, RING, P])
        iota = sb("iota", [P, P])
        ident = sb("ident", [P, P])
        below = sb("below", [P, P])
        ones = sb("ones", [P, P])
        idx = sb("idx", [P, NT], U32)
        local = sb("local", [P, NT])
        totals = sb("totals", [P, NB])
        base = sb("base", [P, NB])
        small = sb("small", [P, 8, NB])
        small_i = sb("small_i", [P, 2, NB], I32)
        seg = sb("seg", [P, TJ])
        seg_k = sb("seg_k", [P, TJ])
        seg_i = sb("seg_i", [P, TJ], I32)
        offs = sb("offs", [1, P * TJ], I32)
        stats = sb("stats", [P, NB, 6])
        mv = sb("mv", [P, NB, 2])
        rstd = sb("rstd", [P, NB])
        nsc = sb("nsc", [P, 3, NB])
        deg = sb("deg", [P, NB])
        rden = sb("rden", [P, NB])
        wg = sb("wg", [P, 2 * KD, D])
        bg = sb("bg", [1, D])
        tmp = sb("tmp", [P, 2, 2 * D])
        lhs = sb("lhs", [P, 2, 2 * KD * P])

        ps = [ctx.enter_context(nc.psum_tensor(f"ps{i}", [P, 512], F32)) for i in range(8)]

        pe, dve, act, pool, sp = (Queue(lane(f"s_{n}")) for n in ("pe", "dve", "act", "pool", "sp"))

        m_src = dve.put(lambda e: e.memset(src_i[:, FULL:T], NB * P))
        m_dst = dve.put(lambda e: e.memset(dst_i[:, FULL:T], 0))
        l_edges = lane("l_edges")
        for t, a in ((src_i, src), (dst_i, dst)):
            got_edges = sp.dma(l_edges, t[:, 0:FULL], a[0:P * FULL].rearrange("(p t) -> p t", p=P))
            if TAIL:
                got_edges = sp.dma(l_edges, t[0:TAIL, FULL:T], a[P * FULL:E].rearrange("(p t) -> p t", t=1),
                                   after=[m_src, m_dst])
        z_node = dve.put(lambda e: e.memset(node[:, NB - 1, :], 0.0))
        l_x = lane("l_x")
        sp.dma(l_x, node[:, 0:NB - 1, :], x[0:(NB - 1) * P, :].rearrange("(b p) d -> p b d", p=P))
        got_x = sp.dma(l_x, node[0:LAST, NB - 1, :], x[(NB - 1) * P:N, :], after=[z_node])
        l_w = lane("l_w")
        sp.dma(l_w, wg[:, 0:KD, :], w_root.rearrange("(k p) n -> p k n", p=P))
        sp.dma(l_w, wg[:, KD:2 * KD, :], w_neigh.rearrange("(k p) n -> p k n", p=P))
        got_wg = sp.dma(l_w, bg[:, :], b_gnn.rearrange("(a n) -> a n", a=1))

        c_iota = pool.put(lambda e: e.iota(iota[:, :], [[1, P]], base=0, channel_multiplier=0,
                                           allow_small_or_imprecise_dtypes=True))
        c_segk = pool.put(lambda e: e.iota(seg_k[:, :], [[1, TJ]], base=0, channel_multiplier=TJ,
                                           allow_small_or_imprecise_dtypes=True))
        c_ones = pool.put(lambda e: e.memset(ones[:, :], 1.0))
        c_zero = pool.put(lambda e: e.memset(local[:, :], 0.0))
        z_id = pool.put(lambda e: e.memset(ident[:, :], 0.0))
        c_id = pool.put(lambda e: e.affine_select(out=ident[:, :], in_=ident[:, :], compare_op=ALU.not_equal,
                                                  fill=1.0, base=0, pattern=[[-1, P]], channel_multiplier=1),
                        after=[z_id])
        c_below = pool.put(lambda e: e.affine_select(out=below[:, :], in_=ones[:, :], compare_op=ALU.is_ge,
                                                     fill=0.0, base=-1, pattern=[[1, P]],
                                                     channel_multiplier=-1), after=[c_ones])
        l_zero = lane("l_zero")
        list_rows = edge_list.rearrange("(p k) a -> p (k a)", p=P)
        list_zeroed = sp.dma(l_zero, list_rows, local[:, :], after=[c_zero])

        v_bi = dve.put(lambda e: e.tensor_scalar(bucket_i, src_i, 7, None, ALU.logical_shift_right),
                       after=[got_edges])
        v_bh = dve.put(lambda e: e.tensor_copy(bucket_h, bucket_i), after=[v_bi])
        v_loc = dve.put(lambda e: e.tensor_scalar(bucket_i, src_i, P - 1, None, ALU.bitwise_and), after=[v_bh])
        v_code = dve.put(lambda e: e.scalar_tensor_tensor(code, dst_i, float(CODE), bucket_i, ALU.mult, ALU.add),
                         after=[v_loc])
        v_code = dve.put(lambda e: e.tensor_scalar(code, code, 1.0, None, ALU.add), after=[v_code])
        v_hot = {}
        v_scan = {}
        for b in range(NB):
            v_hot[b] = dve.put(lambda e, b=b: e.tensor_scalar(hot_h[b % 2], bucket_h, float(b), None, ALU.is_equal),
                               after=[v_bh] + ([v_scan[b - 2]] if b >= 2 else []))
            v_scan[b] = dve.put(lambda e, b=b: e.tensor_tensor_scan(rank[:, b, :], hot_h[b % 2], hot_h[b % 2],
                                                                    0.0, ALU.add, ALU.bypass),
                                after=[v_hot[b]])
        v_tot = dve.put(lambda e: e.tensor_copy(totals[:, :], rank[:, :, T - 1]), after=[v_scan[NB - 1]])
        pe.put(lambda e: e.matmul(ps[0][:, 0:NB], below[:, :], totals[:, :], start=True, stop=True),
               after=[v_tot, c_below])
        t_tot = pe.put(lambda e: e.matmul(ps[1][:, 0:NB], ones[:, :], totals[:, :], start=True, stop=True))
        cnt, nt_f, end_f, start_f = (small[:, i, :] for i in range(4))
        v = dve.put(lambda e: e.tensor_scalar(cnt, ps[1][:, 0:NB], float(P - 1), None, ALU.add), after=[t_tot])
        v = dve.put(lambda e: e.tensor_copy(small_i[:, 0, :], cnt), after=[v])
        v = dve.put(lambda e: e.tensor_scalar(small_i[:, 1, :], small_i[:, 0, :], 7, None, ALU.logical_shift_right),
                    after=[v])
        v = dve.put(lambda e: e.tensor_copy(nt_f, small_i[:, 1, :]), after=[v])
        v_end = dve.put(lambda e: e.tensor_tensor_scan(end_f, nt_f, nt_f, 0.0, ALU.add, ALU.bypass), after=[v])
        v = dve.put(lambda e: e.tensor_tensor(start_f, end_f, nt_f, ALU.subtract), after=[v_end])
        v = dve.put(lambda e: e.tensor_scalar(start_f, start_f, float(P), -1.0, ALU.mult, ALU.add), after=[v])
        v_base = dve.put(lambda e: e.tensor_tensor(base[:, :], ps[0][:, 0:NB], start_f, ALU.add), after=[v])
        v_place = v_base
        for b in range(NB):
            v_h = dve.put(lambda e, b=b: e.tensor_scalar(hot_h[b % 2], bucket_h, float(b), None, ALU.is_equal),
                          after=[v_scan[NB - 1]])
            if b == 0:
                v_place = dve.put(lambda e: e.scalar_tensor_tensor(place, rank[:, 0, :], base[:, 0:1], hot_h[0],
                                                                   ALU.add, ALU.mult), after=[v_h, v_base])
                continue
            v_t = dve.put(lambda e, b=b: e.scalar_tensor_tensor(term, rank[:, b, :], base[:, b:b + 1], hot_h[b % 2],
                                                                ALU.add, ALU.mult), after=[v_h, v_place])
            v_place = dve.put(lambda e: e.tensor_tensor(place, place, term, ALU.add), after=[v_t])
        place_i = bucket_i
        part_i = scratch[:, 2 * T:3 * T].bitcast(I32)
        v = dve.put(lambda e: e.tensor_copy(place_i, place), after=[v_place])
        v = dve.put(lambda e: e.tensor_scalar(part_i, place_i, P - 1, None, ALU.bitwise_and), after=[v])
        v = dve.put(lambda e: e.tensor_scalar(place_i, place_i, 7, None, ALU.logical_shift_right), after=[v])
        addr = edges[:, 0:T].bitcast(U32)
        v_addr = dve.put(lambda e: e.scalar_tensor_tensor(addr, part_i, float(NT), place_i, ALU.mult, ALU.add),
                         after=[v])

        assert TJ * NB <= 4 * D and 5 * T <= NB * (W2 - T // 2) - NB
        seen = tmp[:, :, :].rearrange("p a n -> p (a n)")[:, 0:TJ * NB].rearrange("p (j b) -> p j b", b=NB)
        v = dve.put(lambda e: e.tensor_tensor(seen, end_f.unsqueeze(1).to_broadcast([P, TJ, NB]),
                                              seg_k[:, :].unsqueeze(2).to_broadcast([P, TJ, NB]), ALU.is_le),
                    after=[v_end, c_segk])
        v = dve.put(lambda e: e.tensor_reduce(seg[:, :], seen, AX_X, ALU.add), after=[v])
        v = dve.put(lambda e: e.tensor_scalar(seg[:, :], seg[:, :], float(NB - 1), None, ALU.min), after=[v])
        v_seg = dve.put(lambda e: e.tensor_scalar(seg_i[:, :], seg[:, :], float(W2), None, ALU.mult), after=[v])
        l_seg = lane("l_seg")
        seg_out = sp.dma(l_seg, block_of.rearrange("a (p j) -> p (a j)", p=P), seg_i[:, :], after=[v_seg])
        got_offs = sp.dma(l_seg, offs[:, :], block_of, after=[seg_out])

        l_scatter = lane("l_scatter")
        for t in range(T):
            n = P if t < FULL else TAIL
            scattered = pool.put(lambda e, t=t, n=n: e.indirect_dma_start(
                out=edge_list, out_offset=bass.IndirectOffsetOnAxis(ap=addr[0:n, t:t + 1], axis=0),
                in_=code[0:n, t:t + 1], in_offset=None), after=[v_addr, list_zeroed], lane=l_scatter, by=16)

        def layer_norm_scales(stat_events):
            var, root, quot = nsc[:, 0, :], nsc[:, 1, :], nsc[:, 2, :]
            v0 = dve.put(lambda e: e.tensor_scalar(var, mv[:, :, 1], EPS, None, ALU.add), after=stat_events)
            a0 = act.put(lambda e: e.activation(root, var, ACT.Sqrt), after=[v0])
            v1 = dve.put(lambda e: e.reciprocal(quot, root), after=[a0])
            v1 = dve.put(lambda e: e.tensor_tensor(quot, quot, var, ALU.mult), after=[v1])
            v1 = dve.put(lambda e: e.tensor_tensor(root, root, quot, ALU.add), after=[v1])
            v1 = dve.put(lambda e: e.tensor_scalar(root, root, 0.5, None, ALU.mult), after=[v1])
            return dve.put(lambda e: e.reciprocal(rstd[:, :], root), after=[v1])

        stat = [dve.put(lambda e, b=b: e.bn_stats(stats[:, b, :], node[:, b, :]), after=[got_x]) for b in range(NB)]
        v = [dve.put(lambda e, b=b: e.bn_aggr(mv[:, b, :], stats[:, b, :]), after=[stat[b]]) for b in range(NB)]
        v_rstd = layer_norm_scales(v)
        l_tab = lane("l_tab")
        CH = 7
        for b in range(NB):
            v_xn = dve.put(lambda e, b=b: e.tensor_scalar(node[:, b, :], node[:, b, :], mv[:, b, 0:1], rstd[:, b:b + 1],
                                                          ALU.subtract, ALU.mult), after=[v_rstd])
            if b % CH == CH - 1 or b == NB - 1:
                b0 = b - b % CH
                xn_written = sp.dma(l_tab, xn_table[b0 * P:(b + 1) * P, :].rearrange("(b p) d -> p b d", p=P),
                                    node[:, b0:b + 1, :], after=[v_xn])

        l_list = lane("l_list")
        coded = edges[:, 0:NT]
        listed = sp.dma(l_list, coded, list_rows, after=[scattered])
        ci = edges[:, NT:2 * NT].bitcast(I32)
        cl = edges[:, 2 * NT:3 * NT].bitcast(I32)
        v = dve.put(lambda e: e.tensor_copy(ci, coded), after=[listed, v_place])
        dve.put(lambda e: e.tensor_scalar(cl, ci, CODE - 1, None, ALU.bitwise_and), after=[v])
        v_idx = dve.put(lambda e: e.tensor_scalar(idx[:, :], ci.bitcast(U32), 8, None, ALU.logical_shift_right))
        v_local = dve.put(lambda e: e.tensor_scalar(local[:, :], cl, -1.0, None, ALU.add), after=[v_idx])

        l_row = [lane(f"l_row{i}") for i in range(RING)]

        def edge_pass(table, table_written, width, first, square):
            ready = dve.put(lambda e: e.memset(acc, 0.0), after=first + [scattered])
            hot_at, got, squared, summed, added = {}, {}, {}, {}, {}

            def add(k):
                def issue(e):
                    off = e.value_load(offs[0:1, k:k + 1], min_val=0, max_val=(NB - 1) * W2)
                    block = acc[:, bass.ds(off, width)]
                    return e.tensor_tensor(block, ps[k % BANKS][:, 0:width], block, ALU.add)
                added[k] = dve.put(issue, after=[summed[k], added.get(k - 1, ready), got_offs])

            for k in range(NT + LAG):
                if k < NT:
                    free = [summed[k - RING]] if k >= RING else list(first)
                    got[k] = pool.put(lambda e, k=k: e.indirect_dma_start(
                        out=rows[:, k % RING, 0:D], out_offset=None, in_=table,
                        in_offset=bass.IndirectOffsetOnAxis(ap=idx[:, k:k + 1], axis=0)),
                        after=[v_idx, table_written] + free, lane=l_row[k % RING], by=16)
                    hot_at[k] = dve.put(lambda e, k=k: e.tensor_scalar(
                        hot[:, k % RING, :], iota[:, :], local[:, k:k + 1], None, ALU.is_equal),
                        after=[v_local, c_iota] + free)
                    need = [got[k], hot_at[k]]
                    if square:
                        squared[k] = act.put(lambda e, k=k: e.activation(
                            rows[:, k % RING, D:W2], rows[:, k % RING, 0:D], ACT.Square),
                            after=[got[k]] + free)
                        need.append(squared[k])
                    need += [added[k - BANKS]] if k >= BANKS else list(first)
                    summed[k] = pe.put(lambda e, k=k: e.matmul(
                        ps[k % BANKS][:, 0:width], hot[:, k % RING, :], rows[:, k % RING, 0:width],
                        start=True, stop=True), after=need)
                if k >= LAG:
                    add(k - LAG)
            return added[NT - 1]

        v_one = dve.put(lambda e: e.memset(rows[:, :, D:W1], 1.0), after=[v_addr, v_local])
        sums1 = edge_pass(xn_table, xn_written, W1, [v_one], False)

        by_block = acc.rearrange("p (b w) -> p b w", w=W2)
        v_deg = dve.put(lambda e: e.tensor_copy(deg[:, :], by_block[:, :, D]), after=[sums1])
        v = dve.put(lambda e: e.tensor_scalar(rden[:, :], deg[:, :], 1.0, None, ALU.max), after=[v_deg])
        v_rden = dve.put(lambda e: e.reciprocal(rden[:, :], rden[:, :]), after=[v])
        turned, moved, prod, h_at, h_written = {}, {}, {}, {}, None
        for b in range(NB):
            v_mean = dve.put(lambda e, b=b: e.tensor_scalar(tmp[:, b % 2, 0:D], by_block[:, b, 0:D], rden[:, b:b + 1],
                                                            None, ALU.mult),
                             after=[v_rden] + ([turned[b - 2]] if b >= 2 else []))
            for j in range(2 * KD):
                a = node[:, b, j * P:(j + 1) * P] if j < KD else tmp[:, b % 2, (j - KD) * P:(j - KD + 1) * P]
                turned[b] = pe.put(lambda e, b=b, j=j, a=a: e.transpose(ps[4 + b % 2][:, j * P:(j + 1) * P], a,
                                                                        ident[:, :]),
                                   after=[v_mean, c_id] + ([moved[b - 2]] if b >= 2 else []))
            moved[b] = act.put(lambda e, b=b: e.activation(lhs[:, b % 2, :], ps[4 + b % 2][:, :], ACT.Copy),
                               after=[turned[b]] + ([prod[b - 2]] if b >= 2 else []))
            for j in range(2 * KD):
                pe.put(lambda e, b=b, j=j: e.matmul(ps[6 + b % 2][:, 0:D], lhs[:, b % 2, j * P:(j + 1) * P],
                                                    wg[:, j, :], start=(j == 0), stop=False),
                       after=[moved[b], got_wg] + ([h_at[b - 2]] if b >= 2 else []))
            prod[b] = pe.put(lambda e, b=b: e.matmul(ps[6 + b % 2][:, 0:D], ones[0:1, :], bg[:, :],
                                                     start=False, stop=True))
            h_at[b] = dve.put(lambda e, b=b: e.tensor_scalar(node[:, b, :], ps[6 + b % 2][:, 0:D], 0.0, None, ALU.max),
                              after=[prod[b]])
            if b % CH == CH - 1 or b == NB - 1:
                b0 = b - b % CH
                h_written = sp.dma(l_tab, h_table[b0 * P:(b + 1) * P, :].rearrange("(b p) d -> p b d", p=P),
                                   node[:, b0:b + 1, :], after=[h_at[b], xn_written])

        sums2 = edge_pass(h_table, h_written, W2, [h_at[NB - 1], prod[NB - 1], turned[NB - 1]], True)

        sq = acc.rearrange("p (b w) -> p b w", w=W2)
        l_xr = [lane("l_xr0"), lane("l_xr1")]
        XG = RING
        xr = work[:, :].rearrange("p (h r d) -> p h r d", h=2, r=XG)
        used = {}
        x1_at, tanh_at = {}, {}
        for b in range(NB):
            g, r = divmod(b, XG)
            if r == 0:
                nb = min(XG, NB - b)
                full = min(nb, NB - 1 - b)
                wait_for = [sums2] + ([used[g - 2]] if g >= 2 else [])
                if full:
                    got = sp.dma(l_xr[g % 2], xr[:, g % 2, 0:full, :],
                                 x[b * P:(b + full) * P, :].rearrange("(b p) d -> p b d", p=P), after=wait_for)
                if full < nb:
                    zr = dve.put(lambda e, g=g, full=full: e.memset(xr[:, g % 2, full, :], 0.0), after=wait_for)
                    got = sp.dma(l_xr[g % 2], xr[0:LAST, g % 2, full, :], x[(NB - 1) * P:N, :], after=[zr])
            hd, t1 = tmp[:, b % 2, 0:D], tmp[:, b % 2, D:2 * D]
            a_hd = act.put(lambda e, b=b, hd=hd: e.activation(hd, node[:, b, :], ACT.Copy, scale=deg[:, b:b + 1]),
                           after=[sums2, h_at[NB - 1]] + ([x1_at[b - 2]] if b >= 2 else []))
            v = dve.put(lambda e, b=b, hd=hd, t1=t1: e.scalar_tensor_tensor(t1, sq[:, b, 0:D], -2.0, hd, ALU.mult, ALU.add),
                        after=[a_hd])
            v = dve.put(lambda e, b=b, t1=t1: e.tensor_tensor(t1, t1, node[:, b, :], ALU.mult), after=[v])
            v = dve.put(lambda e, b=b, t1=t1: e.tensor_tensor(t1, t1, sq[:, b, D:W2], ALU.add), after=[v])
            tanh_at[b] = act.put(lambda e, b=b, hd=hd, t1=t1: e.activation(hd, t1, ACT.Tanh, scale=rden[:, b:b + 1]),
                                 after=[v])
            x1_at[b] = dve.put(lambda e, b=b, g=g, r=r, hd=hd: e.tensor_tensor(node[:, b, :], hd, xr[:, g % 2, r, :],
                                                                              ALU.add), after=[tanh_at[b], got])
            used[g] = x1_at[b]
            stat[b] = dve.put(lambda e, b=b: e.bn_stats(stats[:, b, :], node[:, b, :]), after=[x1_at[b]])

        free = spare
        at = 0

        def carve(shape):
            nonlocal at
            n = 1
            for s in shape:
                n *= s
            got = free[:, at:at + n]
            at += n
            return got

        e1 = carve([NE, KD, HID]).rearrange("p (e k n) -> p e k n", e=NE, k=KD)
        e2 = carve([NE, KH, HID]).rearrange("p (e k n) -> p e k n", e=NE, k=KH)
        e3 = carve([NE, KH, D]).rearrange("p (e k n) -> p e k n", e=NE, k=KH)
        r1 = carve([KD, RH]).rearrange("p (k n) -> p k n", k=KD)
        r2 = carve([NE])
        NBR = 2 * NE * KH + 1
        bias_rows = carve([P])[0:NBR, :]
        bias_cols = carve([NBR])
        b1 = bias_cols[:, 0:NE * KH].rearrange("p (e k) -> p e k", e=NE)
        b2 = bias_cols[:, NE * KH:2 * NE * KH].rearrange("p (e k) -> p e k", e=NE)
        br1 = bias_cols[:, 2 * NE * KH:NBR]
        logits = carve([NB, TOP_PAD]).rearrange("p (b n) -> p b n", b=NB)
        top = carve([NB, TOP_PAD]).rearrange("p (b n) -> p b n", b=NB)
        top_i = carve([NB, TOP_PAD]).rearrange("p (b n) -> p b n", b=NB)
        gate = carve([NB, TOP_PAD]).rearrange("p (b n) -> p b n", b=NB)
        pick = carve([NB, TOP_PAD]).rearrange("p (b n) -> p b n", b=NB)
        row_b2 = carve([NE])[0:1, :]
        row_b3 = carve([D])[0:NE, :]
        gateT = carve([GROUP * P])
        assert at <= NB * (W2 - D)
        h1 = edges[:, 0:KH * GROUP * P].rearrange("p (k m) -> p k m", k=KH)
        h2 = edges[:, KH * GROUP * P:2 * KH * GROUP * P].rearrange("p (k m) -> p k m", k=KH)

        done1 = x1_at[NB - 1]
        l_ew = lane("l_ew")
        for k_out, a in ((e1, ew1), (e2, ew2), (e3, ew3)):
            sp.dma(l_ew, k_out, a.rearrange("e (k p) n -> p e k n", p=P), after=[done1])
        sp.dma(l_ew, r1, rw1.rearrange("(k p) n -> p k n", p=P))
        sp.dma(l_ew, r2, rw2)
        sp.dma(l_ew, bias_rows[0:NE * KH, :], eb1.rearrange("e (k p) -> (e k) p", p=P))
        sp.dma(l_ew, bias_rows[NE * KH:2 * NE * KH, :], eb2.rearrange("e (k p) -> (e k) p", p=P))
        sp.dma(l_ew, bias_rows[2 * NE * KH:NBR, :], rb1.rearrange("(a n) -> a n", a=1))
        sp.dma(l_ew, row_b2, rb2.rearrange("(a n) -> a n", a=1))
        got_ew = sp.dma(l_ew, row_b3, eb3)
        t_bias = pe.put(lambda e: e.transpose(ps[7][:, 0:NBR], bias_rows, ident[0:NBR, 0:NBR]),
                        after=[got_ew, h_at[NB - 1]])
        got_bias = act.put(lambda e: e.activation(bias_cols, ps[7][:, 0:NBR], ACT.Copy), after=[t_bias])
        v_lpad = dve.put(lambda e: e.memset(logits, -1e30), after=[done1])

        v = [dve.put(lambda e, b=b: e.bn_aggr(mv[:, b, :], stats[:, b, :]), after=[stat[b]]) for b in range(NB)]
        v_rstd = layer_norm_scales(v)
        turned2, moved2, rh_ps, rh_at, log_at, log_ps = {}, {}, {}, {}, {}, {}
        groups = [range(g, min(g + GROUP, NB)) for g in range(0, NB, GROUP)]
        for g, blocks in enumerate(groups):
            b0, n = blocks[0], len(blocks)
            for b in blocks:
                v_xn = dve.put(lambda e, b=b: e.tensor_scalar(tmp[:, b % 2, 0:D], node[:, b, :], mv[:, b, 0:1],
                                                              rstd[:, b:b + 1], ALU.subtract, ALU.mult),
                               after=[v_rstd, done1] + ([turned2[b - 2]] if b >= 2 else []))
                for k in range(KD):
                    turned2[b] = pe.put(lambda e, b=b, k=k: e.transpose(ps[b % 2][:, k * P:(k + 1) * P],
                                                                       tmp[:, b % 2, k * P:(k + 1) * P], ident[:, :]),
                                        after=[v_xn] + ([moved2[b - 2]] if b >= 2 else [sums2]))
                moved2[b] = act.put(lambda e, b=b: e.activation(xnT[:, b, :, :].rearrange("p k m -> p (k m)"),
                                                                ps[b % 2][:, 0:D], ACT.Copy),
                                    after=[turned2[b], done1])
            for k in range(KD):
                rh_ps[g] = pe.put(lambda e, k=k, b0=b0, n=n, g=g: e.matmul(
                    ps[2 + g % 2][:, 0:n * P], r1[:, k, :], xnT[:, b0:b0 + n, k, :],
                    start=(k == 0), stop=(k == KD - 1)),
                    after=[moved2[blocks[-1]], got_ew] + ([rh_at[g - 2]] if g >= 2 else [sums2]))
            rh_at[g] = act.put(lambda e, g=g, n=n: e.activation(lhs[:, g % 2, 0:n * P], ps[2 + g % 2][:, 0:n * P],
                                                                ACT.Relu, bias=br1),
                               after=[rh_ps[g], prod[NB - 1], got_bias] + ([log_ps[g - 2]] if g >= 2 else []))
            for i in range(n):
                pe.put(lambda e, g=g, i=i: e.matmul(ps[4 + g % 2][:, i * TOP_PAD:i * TOP_PAD + NE],
                                                    lhs[:, g % 2, i * P:(i + 1) * P], r2, start=True, stop=False),
                       after=[rh_at[g]] + ([log_at[g - 2]] if g >= 2 else [h_at[NB - 1], moved[NB - 1]]))
                log_ps[g] = pe.put(lambda e, g=g, i=i: e.matmul(ps[4 + g % 2][:, i * TOP_PAD:i * TOP_PAD + NE],
                                                                ones[0:1, :], row_b2, start=False, stop=True))
            log_at[g] = dve.put(lambda e, g=g, b0=b0, n=n: e.tensor_copy(
                logits[:, b0:b0 + n, 0:NE],
                ps[4 + g % 2][:, 0:n * TOP_PAD].rearrange("p (i m) -> p i m", m=TOP_PAD)[:, :, 0:NE]),
                after=[log_ps[g], v_lpad])

        top_iu = top_i.bitcast(U32)
        v_top = {}
        for b in range(NB):
            v_top[b] = dve.put(lambda e, b=b: e.max(top[:, b, :], logits[:, b, :]), after=[log_at[len(groups) - 1]])
        for b in range(NB):
            v_ti = dve.put(lambda e, b=b: e.max_index(top_iu[:, b, :], top[:, b, :], logits[:, b, :]), after=[v_top[b]])
        maxi = top[:, :, 0:1].to_broadcast([P, NB, TOP_PAD])
        v = dve.put(lambda e: e.tensor_tensor(pick, logits, maxi, ALU.subtract), after=[v_ti])
        a_e = act.put(lambda e: e.activation(pick, pick, ACT.Exp), after=[v])
        s_sum, s_p1, s_p2, s_w1, s_w2, s_d, s_i1, s_i2 = (small[:, i, :] for i in range(8))
        v = dve.put(lambda e: e.tensor_reduce(s_sum, pick[:, :, 0:NE], AX_X, ALU.add), after=[a_e])
        v_p1 = dve.put(lambda e: e.reciprocal(s_p1, s_sum), after=[v])
        v = dve.put(lambda e: e.tensor_tensor(s_d, top[:, :, 1], top[:, :, 0], ALU.subtract))
        a_e = act.put(lambda e: e.activation(s_p2, s_d, ACT.Exp), after=[v])
        v = dve.put(lambda e: e.tensor_tensor(s_p2, s_p2, s_p1, ALU.mult), after=[a_e, v_p1])
        v = dve.put(lambda e: e.tensor_tensor(s_d, s_p2, s_p1, ALU.subtract), after=[v])
        a_e = act.put(lambda e: e.activation(s_w2, s_d, ACT.Exp), after=[v])
        v = dve.put(lambda e: e.tensor_scalar(s_w1, s_w2, 1.0, None, ALU.add), after=[a_e])
        v = dve.put(lambda e: e.reciprocal(s_w1, s_w1), after=[v])
        v = dve.put(lambda e: e.tensor_tensor(s_w2, s_w2, s_w1, ALU.mult), after=[v])
        dve.put(lambda e: e.tensor_copy(s_i1, top_iu[:, :, 0]))
        v = dve.put(lambda e: e.tensor_copy(s_i2, top_iu[:, :, 1]))
        wide = [P, NB, TOP_PAD]
        numbers = iota[:, 0:TOP_PAD].unsqueeze(1).to_broadcast(wide)
        dve.put(lambda e: e.tensor_tensor(gate, numbers, s_i1.unsqueeze(2).to_broadcast(wide), ALU.is_equal), after=[v])
        v = dve.put(lambda e: e.tensor_tensor(pick, numbers, s_i2.unsqueeze(2).to_broadcast(wide), ALU.is_equal))
        dve.put(lambda e: e.tensor_tensor(gate, gate, s_w1.unsqueeze(2).to_broadcast(wide), ALU.mult), after=[v])
        v = dve.put(lambda e: e.tensor_tensor(pick, pick, s_w2.unsqueeze(2).to_broadcast(wide), ALU.mult))
        v_gate = dve.put(lambda e: e.tensor_tensor(gate, gate, pick, ALU.add), after=[v])

        l_out = lane("l_out")
        h1_ps, h1_at, h2_ps, h2_at, y_ps, y_at = {}, {}, {}, {}, {}, {}
        gt_at = {}
        bias_read = None
        router_read = [log_at[len(groups) - 1], rh_at[len(groups) - 1], moved2[NB - 1]]
        n_y = 0
        y_last = {}
        for g, blocks in enumerate(groups):
            b0, n = blocks[0], len(blocks)
            for ex in range(NE):
                s = (g, ex)
                prev = (g, ex - 1) if ex else (g - 1, NE - 1)
                for m in range(KH):
                    for k in range(KD):
                        h1_ps[s, m] = pe.put(lambda e, m=m, k=k, ex=ex, b0=b0, n=n: e.matmul(
                            ps[m][:, 0:n * P], e1[:, ex, k, m * P:(m + 1) * P], xnT[:, b0:b0 + n, k, :],
                            start=(k == 0), stop=(k == KD - 1)),
                            after=[h1_at[prev, m]] if (prev, m) in h1_at else router_read)
                    fr = [h2_ps[prev, KH - 1]] if (prev, KH - 1) in h2_ps else [v_local, scattered]
                    h1_at[s, m] = act.put(lambda e, m=m, ex=ex, n=n: e.activation(
                        h1[:, m, 0:n * P], ps[m][:, 0:n * P], ACT.Relu, bias=b1[:, ex, m:m + 1]),
                        after=[h1_ps[s, m]] + fr)
                for m in range(KH):
                    for k in range(KH):
                        h2_ps[s, m] = pe.put(lambda e, m=m, k=k, ex=ex, n=n: e.matmul(
                            ps[2 + m][:, 0:n * P], e2[:, ex, k, m * P:(m + 1) * P], h1[:, k, 0:n * P],
                            start=(k == 0), stop=(k == KH - 1)),
                            after=[h1_at[s, k]] + ([h2_at[prev, m]] if (prev, m) in h2_at else router_read))
                    fr = [y_last[prev]] if prev in y_last else [v_local, scattered]
                    h2_at[s, m] = act.put(lambda e, m=m, ex=ex, n=n: e.activation(
                        h2[:, m, 0:n * P], ps[2 + m][:, 0:n * P], ACT.Relu, bias=b2[:, ex, m:m + 1]),
                        after=[h2_ps[s, m]] + fr)
                for i, b in enumerate(blocks):
                    bank = 4 + n_y % 3
                    for k in range(KH):
                        y = pe.put(lambda e, i=i, k=k, ex=ex, bank=bank: e.matmul(
                            ps[bank][:, 0:D], h2[:, k, i * P:(i + 1) * P], e3[:, ex, k, :],
                            start=(k == 0), stop=(k == KH - 1)),
                            after=[h2_at[s, k]] + ([y_at[n_y - 3]] if n_y >= 3 else router_read))
                    y_last[s] = y
                    y_at[n_y] = dve.put(lambda e, b=b, ex=ex, bank=bank: e.scalar_tensor_tensor(
                        node[:, b, :], ps[bank][:, 0:D], gate[:, b, ex:ex + 1], node[:, b, :], ALU.mult, ALU.add),
                        after=[y, v_gate] + ([y_at[n_y - n]] if n_y >= n else []))
                    n_y += 1
            for i, b in enumerate(blocks):
                t = pe.put(lambda e, i=i, b=b: e.transpose(ps[7][0:NE, i * P:(i + 1) * P], gate[:, b, 0:NE],
                                                           ident[:, :]),
                           after=[v_gate] + ([bias_read] if bias_read else []))
            gt_at[g] = act.put(lambda e, n=n: e.activation(gateT[0:NE, 0:n * P], ps[7][0:NE, 0:n * P], ACT.Copy),
                               after=[t])
            for i, b in enumerate(blocks):
                bank = 4 + n_y % 3
                y = pe.put(lambda e, i=i, bank=bank: e.matmul(ps[bank][:, 0:D], gateT[0:NE, i * P:(i + 1) * P],
                                                              row_b3, start=True, stop=True),
                           after=[gt_at[g], y_at[n_y - 3]])
                bias_read = y
                y_at[n_y] = dve.put(lambda e, b=b, bank=bank: e.tensor_tensor(
                    node[:, b, :], ps[bank][:, 0:D], node[:, b, :], ALU.add), after=[y, y_at[n_y - n]])
                n_y += 1
            full = n if blocks[-1] < NB - 1 else n - 1
            if full:
                stored = sp.dma(l_out, out[b0 * P:(b0 + full) * P, :].rearrange("(b p) d -> p b d", p=P),
                                node[:, b0:b0 + full, :], after=[y_at[n_y - 1]])
            if full < n:
                stored = sp.dma(l_out, out[(NB - 1) * P:N, :], node[0:LAST, NB - 1, :], after=[y_at[n_y - 1]])
        for done in (stored, h_written, seg_out, list_zeroed, scattered):
            sp.wait(done)

        block = ctx.enter_context(nc.Block())

        @block.sync
        def _(e):
            sp.run(e)

        @block.tensor
        def _(e):
            pe.run(e)

        @block.vector
        def _(e):
            dve.run(e)

        @block.scalar
        def _(e):
            act.run(e)

        @block.gpsimd
        def _(e):
            pool.run(e)


_INS = ["x", "src", "dst", "L0_gnn_W_root", "L0_gnn_W_neigh", "L0_gnn_b", "L0_ffn_router_w1", "L0_ffn_router_b1",
        "L0_ffn_router_w2", "L0_ffn_router_b2", "L0_ffn_expert_w1", "L0_ffn_expert_b1", "L0_ffn_expert_w2",
        "L0_ffn_expert_b2", "L0_ffn_expert_w3", "L0_ffn_expert_b3"]


def kernel(**inputs):
    import numpy as np
    import concourse.bacc as bacc
    from concourse.bass_utils import run_bass_kernel_spmd

    nc = bacc.Bacc("TRN2", target_bir_lowering=False, num_devices=1)
    arrays, args = {}, []
    for name in _INS:
        a = np.ascontiguousarray(inputs[name])
        arrays[f"in_{name}"] = a
        args.append(nc.dram_tensor(f"in_{name}", a.shape, mybir.dt.from_np(a.dtype), kind="ExternalInput").ap())
    args.append(nc.dram_tensor("result", arrays["in_x"].shape, F32, kind="ExternalOutput").ap())
    gnn_moe_kernel(nc, *args)
    done = run_bass_kernel_spmd(nc, [arrays], core_ids=[0])
    return done.results[0]["result"]
```

```python
from contextlib import ExitStack

import concourse.bass as bass
from concourse import mybir

F32 = mybir.dt.float32
F16 = mybir.dt.float16
I32 = mybir.dt.int32
U32 = mybir.dt.uint32
ALU = mybir.AluOpType
ACT = mybir.ActivationFunctionType
AX_X = mybir.AxisListType.X

P = 128
EPS = 1e-5
SQUARES = 6
HOTS = 6
BANKS = 4
LAG = 3
TOP_PAD = 8
GROUP = 4


class Lane:

    def __init__(self, sem):
        self.sem, self.value = sem, 0

    def add(self, by):
        self.value += by
        return (self, self.value)


class Queue:

    def __init__(self, lane):
        self.steps, self.lane, self.seen = [], lane, {}

    def put(self, issue, after=(), lane=None, by=1):
        waits = []
        for other, value in after:
            if self.seen.get(id(other), 0) < value:
                self.seen[id(other)] = value
                waits.append((other.sem, value))
        lane = lane or self.lane
        self.steps.append((waits, issue, lane.sem, by))
        return lane.add(by)

    def dma(self, lane, out, in_, after=()):
        return self.put(lambda e: e.dma_start(out, in_), after, lane, 16)

    def prepare(self, issue, after=()):
        self.steps.append(([(other.sem, value) for other, value in after], issue, None, 0))

    def wait(self, event):
        self.steps.append(([(event[0].sem, event[1])], None, None, 0))

    def run(self, engine):
        for waits, issue, sem, by in self.steps:
            for other, value in waits:
                engine.wait_ge(other, value)
            if sem is not None:
                issue(engine).then_inc(sem, by)
            elif issue is not None:
                issue(engine)


def gnn_moe_kernel(nc, x, src, dst, w_root, w_neigh, b_gnn, rw1, rb1, rw2, rb2,
                   ew1, eb1, ew2, eb2, ew3, eb3, out):
    N, D = x.shape
    E = src.shape[0]
    NE, _, HID = ew1.shape
    RH = rw1.shape[1]
    KD = D // P
    KH = HID // P
    NB = -(-N // P)
    LAST = N - (NB - 1) * P
    FULL, TAIL = divmod(E, P)
    T = FULL + (TAIL > 0)
    NT = (E + NB * (P - 1)) // P
    TJ = -(-NT // P)
    W1 = D + 2
    W2 = 2 * D
    CODE = 256

    with ExitStack() as ctx:
        def sb(name, shape, dt=F32):
            return ctx.enter_context(nc.sbuf_tensor(name, shape, dt))

        def lane(name):
            return Lane(ctx.enter_context(nc.semaphore(name)))

        xn_table = nc.dram_tensor("xn_table", [NB * P, D], F32, kind="Internal").ap()
        h_table = nc.dram_tensor("h_table", [NB * P, D], F32, kind="Internal").ap()
        edge_list = nc.dram_tensor("edge_list", [P * NT, 1], F32, kind="Internal").ap()
        block_of = nc.dram_tensor("block_of", [1, P * TJ], I32, kind="Internal").ap()

        node = sb("node", [P, NB, D])
        big = sb("big", [P, NB * W2])
        rank = big[:, 0:NB * T // 2 + 1].bitcast(F16)[:, 0:NB * T].rearrange("p (b t) -> p b t", b=NB)
        acc = big[:, :]
        xnT = big[:, 0:NB * D].rearrange("p (b k m) -> p b k m", b=NB, k=KD)
        spare = big[:, NB * D:]
        SLOTS = 24
        arena = sb("arena", [P, SLOTS * W1 + 2 * D])
        edges = arena[:, 0:4 * T]
        src_i = edges[:, 0:T].bitcast(I32)
        dst_i = edges[:, T:2 * T].bitcast(I32)
        code = edges[:, 2 * T:3 * T]
        place = edges[:, 3 * T:4 * T]
        scratch = big[:, NB * T // 2 + 1:]
        bucket_i = scratch[:, 0:T].bitcast(I32)
        bucket_h = scratch[:, T:2 * T].bitcast(F16)[:, 0:T]
        hot_h = [scratch[:, (2 + i) * T:(3 + i) * T].bitcast(F16)[:, 0:T] for i in range(2)]
        term = scratch[:, 4 * T:5 * T]
        rows1 = arena[:, 0:SLOTS * W1].rearrange("p (r w) -> p r w", w=W1)
        rows2 = arena[:, 0:SLOTS * D].rearrange("p (r w) -> p r w", w=D)
        hot = sb("hot", [P, HOTS, P])
        iota = sb("iota", [P, P])
        ident = sb("ident", [P, P])
        below = sb("below", [P, P])
        ones = sb("ones", [P, P])
        idx = sb("idx", [P, NT], U32)
        local = sb("local", [P, NT])
        totals = sb("totals", [P, NB])
        base = sb("base", [P, NB])
        small = sb("small", [P, 8, NB])
        small_i = sb("small_i", [P, 2, NB], I32)
        seg = sb("seg", [P, TJ])
        seg_k = sb("seg_k", [P, TJ])
        seg_i = sb("seg_i", [P, TJ], I32)
        offs = sb("offs", [1, P * TJ], I32)
        stats = sb("stats", [P, NB, 6])
        mv = sb("mv", [P, NB, 2])
        rstd = sb("rstd", [P, NB])
        nsc = sb("nsc", [P, 3, NB])
        deg = sb("deg", [P, NB])
        rden = sb("rden", [P, NB])
        wg = sb("wg", [P, 2 * KD, D])
        bg = sb("bg", [1, D])
        tmp = sb("tmp", [P, 2, 2 * D])
        lhs = sb("lhs", [P, 2, 2 * KD * P])

        ps = [ctx.enter_context(nc.psum_tensor(f"ps{i}", [P, 512], F32)) for i in range(8)]

        pe, dve, act, pool, sp = (Queue(lane(f"s_{n}")) for n in ("pe", "dve", "act", "pool", "sp"))

        m_src = dve.put(lambda e: e.memset(src_i[:, FULL:T], NB * P))
        m_dst = dve.put(lambda e: e.memset(dst_i[:, FULL:T], 0))
        l_edges = lane("l_edges")
        for t, a in ((src_i, src), (dst_i, dst)):
            got_edges = sp.dma(l_edges, t[:, 0:FULL], a[0:P * FULL].rearrange("(p t) -> p t", p=P))
            if TAIL:
                got_edges = sp.dma(l_edges, t[0:TAIL, FULL:T], a[P * FULL:E].rearrange("(p t) -> p t", t=1),
                                   after=[m_src, m_dst])
        z_node = dve.put(lambda e: e.memset(node[:, NB - 1, :], 0.0))
        l_x = lane("l_x")
        sp.dma(l_x, node[:, 0:NB - 1, :], x[0:(NB - 1) * P, :].rearrange("(b p) d -> p b d", p=P))
        got_x = sp.dma(l_x, node[0:LAST, NB - 1, :], x[(NB - 1) * P:N, :], after=[z_node])
        l_w = lane("l_w")
        sp.dma(l_w, wg[:, 0:KD, :], w_root.rearrange("(k p) n -> p k n", p=P))
        sp.dma(l_w, wg[:, KD:2 * KD, :], w_neigh.rearrange("(k p) n -> p k n", p=P))
        got_wg = sp.dma(l_w, bg[:, :], b_gnn.rearrange("(a n) -> a n", a=1))

        c_iota = pool.put(lambda e: e.iota(iota[:, :], [[1, P]], base=0, channel_multiplier=0,
                                           allow_small_or_imprecise_dtypes=True))
        c_segk = pool.put(lambda e: e.iota(seg_k[:, :], [[1, TJ]], base=0, channel_multiplier=TJ,
                                           allow_small_or_imprecise_dtypes=True))
        c_ones = pool.put(lambda e: e.memset(ones[:, :], 1.0))
        c_zero = pool.put(lambda e: e.memset(local[:, :], 0.0))
        z_id = pool.put(lambda e: e.memset(ident[:, :], 0.0))
        c_id = pool.put(lambda e: e.affine_select(out=ident[:, :], in_=ident[:, :], compare_op=ALU.not_equal,
                                                  fill=1.0, base=0, pattern=[[-1, P]], channel_multiplier=1),
                        after=[z_id])
        c_below = pool.put(lambda e: e.affine_select(out=below[:, :], in_=ones[:, :], compare_op=ALU.is_ge,
                                                     fill=0.0, base=-1, pattern=[[1, P]],
                                                     channel_multiplier=-1), after=[c_ones])
        l_zero = lane("l_zero")
        list_rows = edge_list.rearrange("(p k) a -> p (k a)", p=P)
        list_zeroed = sp.dma(l_zero, list_rows, local[:, :], after=[c_zero])

        v_bi = dve.put(lambda e: e.tensor_scalar(bucket_i, src_i, 7, None, ALU.logical_shift_right),
                       after=[got_edges])
        v_bh = dve.put(lambda e: e.tensor_copy(bucket_h, bucket_i), after=[v_bi])
        v_loc = dve.put(lambda e: e.tensor_scalar(bucket_i, src_i, P - 1, None, ALU.bitwise_and), after=[v_bh])
        v_code = dve.put(lambda e: e.scalar_tensor_tensor(code, dst_i, float(CODE), bucket_i, ALU.mult, ALU.add),
                         after=[v_loc])
        v_code = dve.put(lambda e: e.tensor_scalar(code, code, 1.0, None, ALU.add), after=[v_code])
        v_hot = {}
        v_scan = {}
        for b in range(NB):
            v_hot[b] = dve.put(lambda e, b=b: e.tensor_scalar(hot_h[b % 2], bucket_h, float(b), None, ALU.is_equal),
                               after=[v_bh] + ([v_scan[b - 2]] if b >= 2 else []))
            v_scan[b] = dve.put(lambda e, b=b: e.tensor_tensor_scan(rank[:, b, :], hot_h[b % 2], hot_h[b % 2],
                                                                    0.0, ALU.add, ALU.bypass),
                                after=[v_hot[b]])
        v_tot = dve.put(lambda e: e.tensor_copy(totals[:, :], rank[:, :, T - 1]), after=[v_scan[NB - 1]])
        pe.put(lambda e: e.matmul(ps[0][:, 0:NB], below[:, :], totals[:, :], start=True, stop=True),
               after=[v_tot, c_below])
        t_tot = pe.put(lambda e: e.matmul(ps[1][:, 0:NB], ones[:, :], totals[:, :], start=True, stop=True))
        cnt, nt_f, end_f, start_f = (small[:, i, :] for i in range(4))
        v = dve.put(lambda e: e.tensor_scalar(cnt, ps[1][:, 0:NB], float(P - 1), None, ALU.add), after=[t_tot])
        v = dve.put(lambda e: e.tensor_copy(small_i[:, 0, :], cnt), after=[v])
        v = dve.put(lambda e: e.tensor_scalar(small_i[:, 1, :], small_i[:, 0, :], 7, None, ALU.logical_shift_right),
                    after=[v])
        v = dve.put(lambda e: e.tensor_copy(nt_f, small_i[:, 1, :]), after=[v])
        v_end = dve.put(lambda e: e.tensor_tensor_scan(end_f, nt_f, nt_f, 0.0, ALU.add, ALU.bypass), after=[v])
        v = dve.put(lambda e: e.tensor_tensor(start_f, end_f, nt_f, ALU.subtract), after=[v_end])
        v = dve.put(lambda e: e.tensor_scalar(start_f, start_f, float(P), -1.0, ALU.mult, ALU.add), after=[v])
        v_base = dve.put(lambda e: e.tensor_tensor(base[:, :], ps[0][:, 0:NB], start_f, ALU.add), after=[v])
        v_place = v_base
        for b in range(NB):
            v_h = dve.put(lambda e, b=b: e.tensor_scalar(hot_h[b % 2], bucket_h, float(b), None, ALU.is_equal),
                          after=[v_scan[NB - 1]])
            if b == 0:
                v_place = dve.put(lambda e: e.scalar_tensor_tensor(place, rank[:, 0, :], base[:, 0:1], hot_h[0],
                                                                   ALU.add, ALU.mult), after=[v_h, v_base])
                continue
            v_t = dve.put(lambda e, b=b: e.scalar_tensor_tensor(term, rank[:, b, :], base[:, b:b + 1], hot_h[b % 2],
                                                                ALU.add, ALU.mult), after=[v_h, v_place])
            v_place = dve.put(lambda e: e.tensor_tensor(place, place, term, ALU.add), after=[v_t])
        place_i = bucket_i
        part_i = scratch[:, 2 * T:3 * T].bitcast(I32)
        v = dve.put(lambda e: e.tensor_copy(place_i, place), after=[v_place])
        v = dve.put(lambda e: e.tensor_scalar(part_i, place_i, P - 1, None, ALU.bitwise_and), after=[v])
        v = dve.put(lambda e: e.tensor_scalar(place_i, place_i, 7, None, ALU.logical_shift_right), after=[v])
        addr = edges[:, 0:T].bitcast(U32)
        v_addr = dve.put(lambda e: e.scalar_tensor_tensor(addr, part_i, float(NT), place_i, ALU.mult, ALU.add),
                         after=[v])

        assert TJ * NB <= 4 * D and 5 * T <= NB * (W2 - T // 2) - NB
        seen = tmp[:, :, :].rearrange("p a n -> p (a n)")[:, 0:TJ * NB].rearrange("p (j b) -> p j b", b=NB)
        v = dve.put(lambda e: e.tensor_tensor(seen, end_f.unsqueeze(1).to_broadcast([P, TJ, NB]),
                                              seg_k[:, :].unsqueeze(2).to_broadcast([P, TJ, NB]), ALU.is_le),
                    after=[v_end, c_segk])
        v = dve.put(lambda e: e.tensor_reduce(seg[:, :], seen, AX_X, ALU.add), after=[v])
        v = dve.put(lambda e: e.tensor_scalar(seg[:, :], seg[:, :], float(NB - 1), None, ALU.min), after=[v])
        v_seg = dve.put(lambda e: e.tensor_scalar(seg_i[:, :], seg[:, :], float(W2), None, ALU.mult), after=[v])
        l_seg = lane("l_seg")
        seg_out = sp.dma(l_seg, block_of.rearrange("a (p j) -> p (a j)", p=P), seg_i[:, :], after=[v_seg])
        got_offs = sp.dma(l_seg, offs[:, :], block_of, after=[seg_out])

        l_scatter = lane("l_scatter")
        for t in range(T):
            n = P if t < FULL else TAIL
            scattered = pool.put(lambda e, t=t, n=n: e.indirect_dma_start(
                out=edge_list, out_offset=bass.IndirectOffsetOnAxis(ap=addr[0:n, t:t + 1], axis=0),
                in_=code[0:n, t:t + 1], in_offset=None), after=[v_addr, list_zeroed], lane=l_scatter, by=16)

        def layer_norm_scales(stat_events, b0=0, n=NB):
            var, root, quot = (nsc[:, i, b0:b0 + n] for i in range(3))
            v0 = dve.put(lambda e: e.tensor_scalar(var, mv[:, b0:b0 + n, 1], EPS, None, ALU.add), after=stat_events)
            a0 = act.put(lambda e: e.activation(root, var, ACT.Sqrt), after=[v0])
            v1 = dve.put(lambda e: e.reciprocal(quot, root), after=[a0])
            v1 = dve.put(lambda e: e.tensor_tensor(quot, quot, var, ALU.mult), after=[v1])
            v1 = dve.put(lambda e: e.tensor_tensor(root, root, quot, ALU.add), after=[v1])
            v1 = dve.put(lambda e: e.tensor_scalar(root, root, 0.5, None, ALU.mult), after=[v1])
            return dve.put(lambda e: e.reciprocal(rstd[:, b0:b0 + n], root), after=[v1])

        stat = [dve.put(lambda e, b=b: e.bn_stats(stats[:, b, :], node[:, b, :]), after=[got_x]) for b in range(NB)]
        v = [dve.put(lambda e, b=b: e.bn_aggr(mv[:, b, :], stats[:, b, :]), after=[stat[b]]) for b in range(NB)]
        v_rstd = layer_norm_scales(v)
        l_tab = lane("l_tab")
        CH = 7
        xn_at = {}

        def root_product(b):
            for j in range(KD):
                pe.put(lambda e, b=b, j=j: e.matmul(ps[6 + b % 2][:, 0:D], lhs[:, b % 2, j * P:(j + 1) * P],
                                                    wg[:, j, :], start=(j == 0), stop=False),
                       after=[moved[b], got_wg] + ([r_at[b - 2]] if b >= 2 else []))
            prod[b] = pe.put(lambda e, b=b: e.matmul(ps[6 + b % 2][:, 0:D], ones[0:1, :], bg[:, :],
                                                     start=False, stop=True))
            r_at[b] = act.put(lambda e, b=b: e.activation(node[:, b, :], ps[6 + b % 2][:, 0:D], ACT.Copy),
                              after=[prod[b], xn_written])

        for b in range(NB):
            xn_at[b] = v_xn = dve.put(lambda e, b=b: e.tensor_scalar(node[:, b, :], node[:, b, :], mv[:, b, 0:1], rstd[:, b:b + 1],
                                                          ALU.subtract, ALU.mult), after=[v_rstd])
            if b % CH == CH - 1 or b == NB - 1:
                b0 = b - b % CH
                xn_written = sp.dma(l_tab, xn_table[b0 * P:(b + 1) * P, :].rearrange("(b p) d -> p b d", p=P),
                                    node[:, b0:b + 1, :], after=[v_xn])

        turned, moved, prod, r_at = {}, {}, {}, {}
        for b in range(NB):
            for j in range(KD):
                turned[b] = pe.put(lambda e, b=b, j=j: e.transpose(ps[4 + b % 2][:, j * P:(j + 1) * P],
                                                                   node[:, b, j * P:(j + 1) * P], ident[:, :]),
                                   after=[xn_at[b], c_id] + ([moved[b - 2]] if b >= 2 else []))
            moved[b] = act.put(lambda e, b=b: e.activation(lhs[:, b % 2, 0:D], ps[4 + b % 2][:, 0:D], ACT.Copy),
                               after=[turned[b]] + ([prod[b - 2]] if b >= 2 else []))
            if b:
                root_product(b - 1)
        root_product(NB - 1)

        l_list = lane("l_list")
        coded = edges[:, 0:NT]
        listed = sp.dma(l_list, coded, list_rows, after=[scattered])
        ci = edges[:, NT:2 * NT].bitcast(I32)
        cl = edges[:, 2 * NT:3 * NT].bitcast(I32)
        v = dve.put(lambda e: e.tensor_copy(ci, coded), after=[listed, v_place])
        dve.put(lambda e: e.tensor_scalar(cl, ci, CODE - 1, None, ALU.bitwise_and), after=[v])
        v_idx = dve.put(lambda e: e.tensor_scalar(idx[:, :], ci.bitcast(U32), 8, None, ALU.logical_shift_right))
        v_local = dve.put(lambda e: e.tensor_scalar(local[:, :], cl, -1.0, None, ALU.add), after=[v_idx])

        l_row = [lane(f"l_row{i}") for i in range(SLOTS)]

        def edge_pass(table, table_written, width, first, square):
            ready = dve.put(lambda e: e.memset(acc, 0.0), after=first + [scattered])
            ring = SLOTS - SQUARES if square else SLOTS
            hot_at, got, squared, summed, added, place_of = {}, {}, {}, {}, {}, {}

            def load_offset(k):
                def issue(e):
                    place_of[k] = nc.values_load(
                        offs[0:1, k:k + 1], engines=[mybir.EngineType.DVE], min_val=0, max_val=(NB - 1) * W2,
                        skip_runtime_bounds_check_because="the block's number was limited to NB - 1")
                dve.prepare(issue, after=[got_offs] if k == 0 else [])

            def add(k):
                def issue(e):
                    block = acc[:, bass.ds(place_of[k], width)]
                    return e.tensor_tensor(block, ps[k % BANKS][:, 0:width], block, ALU.add)
                added[k] = dve.put(issue, after=[summed[k], added.get(k - 1, ready)])

            for k in range(NT + LAG):
                if LAG <= k:
                    load_offset(k - LAG)
                if k < NT:
                    def free(depth):
                        return [summed[k - depth]] if k >= depth else list(first)
                    slot, sq = k % ring, ring + k % SQUARES
                    row = rows2[:, slot, :] if square else rows1[:, slot, 0:D]
                    got[k] = pool.put(lambda e, k=k, row=row: e.indirect_dma_start(
                        out=row, out_offset=None, in_=table,
                        in_offset=bass.IndirectOffsetOnAxis(ap=idx[:, k:k + 1], axis=0)),
                        after=[v_idx, table_written] + free(ring), lane=l_row[slot], by=16)
                    hot_at[k] = dve.put(lambda e, k=k: e.tensor_scalar(
                        hot[:, k % HOTS, :], iota[:, :], local[:, k:k + 1], None, ALU.is_equal),
                        after=[v_local, c_iota] + free(HOTS))
                    need = [got[k], hot_at[k]]
                    moving, total = rows1[:, slot, :], ps[k % BANKS][:, 0:width]
                    if square:
                        squared[k] = act.put(lambda e, row=row, sq=sq: e.activation(rows2[:, sq, :], row, ACT.Square),
                                             after=[got[k]] + free(SQUARES))
                        need.append(squared[k])
                        moving = rows2[:, slot:sq + 1:sq - slot, :]
                        total = total.rearrange("p (a w) -> p a w", a=2)
                    need += [added[k - BANKS]] if k >= BANKS else list(first)
                    summed[k] = pe.put(lambda e, k=k, moving=moving, total=total: e.matmul(
                        total, hot[:, k % HOTS, :], moving, start=True, stop=True), after=need)
                if k >= LAG:
                    add(k - LAG)
            return added[NT - 1]

        v_one = dve.put(lambda e: e.memset(rows1[:, :, D:W1], 1.0), after=[v_addr, v_local])
        sums1 = edge_pass(xn_table, xn_written, W1, [v_one, r_at[NB - 1]], False)

        by_block = acc.rearrange("p (b w) -> p b w", w=W2)
        v_deg = dve.put(lambda e: e.tensor_copy(deg[:, :], by_block[:, :, D]), after=[sums1])
        v = dve.put(lambda e: e.tensor_scalar(rden[:, :], deg[:, :], 1.0, None, ALU.max), after=[v_deg])
        v_rden = dve.put(lambda e: e.reciprocal(rden[:, :], rden[:, :]), after=[v])
        turned, moved, prod, h_at, v_mean, h_written = {}, {}, {}, {}, {}, None
        HD = 3
        mean = arena[:, 0:HD * D].rearrange("p (r d) -> p r d", d=D)
        left = arena[:, HD * D:2 * HD * D].rearrange("p (r d) -> p r d", d=D)
        pre = arena[:, 2 * HD * D:3 * HD * D].rearrange("p (r d) -> p r d", d=D)

        def neighbour_product(b):
            nonlocal h_written
            for j in range(KD):
                prod[b] = pe.put(lambda e, b=b, j=j: e.matmul(
                    ps[HD + b % HD][:, 0:D], left[:, b % HD, j * P:(j + 1) * P], wg[:, KD + j, :],
                    start=(j == 0), stop=(j == KD - 1)), after=[moved[b]] + ([h_at[b - HD]] if b >= HD else []))
            v_pre = dve.put(lambda e, b=b: e.tensor_tensor(pre[:, b % HD, :], ps[HD + b % HD][:, 0:D],
                                                           node[:, b, :], ALU.add),
                            after=[prod[b], r_at[NB - 1]] + ([h_at[b - HD]] if b >= HD else []))
            h_at[b] = act.put(lambda e, b=b: e.activation(node[:, b, :], pre[:, b % HD, :], ACT.Relu),
                              after=[v_pre])
            if b % CH == CH - 1 or b == NB - 1:
                b0 = b - b % CH
                h_written = sp.dma(l_tab, h_table[b0 * P:(b + 1) * P, :].rearrange("(b p) d -> p b d", p=P),
                                   node[:, b0:b + 1, :], after=[h_at[b], xn_written])

        for b in range(NB + 1):
            if b < NB:
                v_mean[b] = dve.put(lambda e, b=b: e.tensor_scalar(
                    mean[:, b % HD, :], by_block[:, b, 0:D], rden[:, b:b + 1], None, ALU.mult),
                    after=[v_rden] + ([turned[b - HD]] if b >= HD else []))
                for j in range(KD):
                    turned[b] = pe.put(lambda e, b=b, j=j: e.transpose(
                        ps[b % HD][:, j * P:(j + 1) * P], mean[:, b % HD, j * P:(j + 1) * P], ident[:, :]),
                        after=[v_mean[b]] + ([moved[b - HD]] if b >= HD else [sums1]))
                moved[b] = act.put(lambda e, b=b: e.activation(left[:, b % HD, :], ps[b % HD][:, 0:D], ACT.Copy),
                                   after=[turned[b], sums1] + ([prod[b - HD]] if b >= HD else []))
            if b:
                neighbour_product(b - 1)

        sums2 = edge_pass(h_table, h_written, W2, [h_at[NB - 1], prod[NB - 1]], True)

        sq = acc.rearrange("p (b w) -> p b w", w=W2)
        XG = 7
        l_xr = [lane("l_xr0"), lane("l_xr1")]
        xr = arena[:, 0:2 * XG * D].rearrange("p (h r d) -> p h r d", h=2, r=XG)
        XD = 4
        mid = arena[:, 2 * XG * D:2 * XG * D + 2 * XD * D].rearrange("p (r a d) -> p r a d", a=2, d=D)
        used, x1_at, tanh_at, prod_at, got_xr, stat = {}, {}, {}, {}, {}, {}

        def finish_x1(b):
            g, i = divmod(b, XG)
            hd, t1 = mid[:, b % XD, 0, :], mid[:, b % XD, 1, :]
            v = dve.put(lambda e: e.tensor_tensor(t1, t1, sq[:, b, D:W2], ALU.add), after=[prod_at[b]])
            tanh_at[b] = act.put(lambda e: e.activation(hd, t1, ACT.Tanh, scale=rden[:, b:b + 1]), after=[v])
            if b:
                add_x(b - 1)

        def add_x(b):
            g, i = divmod(b, XG)
            used[g] = x1_at[b] = pool.put(lambda e: e.tensor_tensor(
                node[:, b, :], mid[:, b % XD, 0, :], xr[:, g % 2, i, :], ALU.add),
                after=[tanh_at[b], got_xr[g], prod_at[b]])
            stat[b] = dve.put(lambda e: e.bn_stats(stats[:, b, :], node[:, b, :]), after=[x1_at[b]])

        for g in range(-(-NB // XG)):
            b, nb = g * XG, min(XG, NB - g * XG)
            full = min(nb, NB - 1 - b)
            def reload(g=g, b=b, nb=nb, full=full):
                wait_for = [used[g - 2]] if g >= 2 else [sums2]
                if full:
                    got_xr[g] = sp.dma(l_xr[g % 2], xr[:, g % 2, 0:full, :],
                                       x[b * P:(b + full) * P, :].rearrange("(b p) d -> p b d", p=P), after=wait_for)
                if full < nb:
                    zr = pool.put(lambda e: e.memset(xr[:, g % 2, full, :], 0.0), after=wait_for)
                    got_xr[g] = sp.dma(l_xr[g % 2], xr[0:LAST, g % 2, full, :], x[(NB - 1) * P:N, :], after=[zr])
            reload()
            for b in range(b, b + nb):
                hd, t1 = mid[:, b % XD, 0, :], mid[:, b % XD, 1, :]
                a_hd = act.put(lambda e, b=b, hd=hd: e.activation(hd, node[:, b, :], ACT.Copy, scale=deg[:, b:b + 1]),
                               after=[sums2, h_at[NB - 1]] + ([x1_at[b - XD]] if b >= XD else []))
                v = dve.put(lambda e, b=b, hd=hd, t1=t1: e.scalar_tensor_tensor(
                    t1, sq[:, b, 0:D], -2.0, hd, ALU.mult, ALU.add),
                    after=[a_hd] + ([tanh_at[b - XD]] if b >= XD else []))
                p_ = pool.put(lambda e, b=b, t1=t1: e.tensor_tensor(t1, t1, node[:, b, :], ALU.mult), after=[v])
                prod_at[b] = p_
                if b >= 1:
                    finish_x1(b - 1)
        finish_x1(NB - 1)
        add_x(NB - 1)

        at = 0

        def carve(shape):
            nonlocal at
            n = 1
            for d in shape:
                n *= d
            at += n
            return big[:, at - n:at]

        e1 = carve([NE, KD, HID]).rearrange("p (e k n) -> p e k n", e=NE, k=KD)
        e2 = carve([NE, KH, HID]).rearrange("p (e k n) -> p e k n", e=NE, k=KH)
        e3 = carve([NE, KH, D]).rearrange("p (e k n) -> p e k n", e=NE, k=KH)
        r1 = carve([KD, RH]).rearrange("p (k n) -> p k n", k=KD)
        r2 = carve([NE])
        NBR = 2 * NE * KH + 1
        bias_rows = carve([P])[0:NBR, :]
        row_b2 = carve([NE])[0:1, :]
        row_b3 = carve([D])[0:NE, :]
        loaded = -(-at // W2)
        bias_cols = carve([NBR])
        b1 = bias_cols[:, 0:NE * KH].rearrange("p (e k) -> p e k", e=NE)
        b2 = bias_cols[:, NE * KH:2 * NE * KH].rearrange("p (e k) -> p e k", e=NE)
        br1 = bias_cols[:, 2 * NE * KH:NBR]
        wide = [P, GROUP, TOP_PAD]

        def carve_small():
            return carve(wide[1:]).rearrange("p (b n) -> p b n", b=GROUP)

        logits = carve_small()
        top, top_i, pick = carve_small(), carve_small(), carve_small()
        gates = [carve_small(), carve_small()]
        scal = carve([8, GROUP]).rearrange("p (a b) -> p a b", a=8)
        gateT = carve([GROUP * P])
        xnT = [carve([GROUP, KD, P]).rearrange("p (b k m) -> p b k m", b=GROUP, k=KD) for _ in range(2)]
        rh = carve([GROUP * P])
        h1 = carve([KH, GROUP * P]).rearrange("p (k m) -> p k m", k=KH)
        h2 = carve([KH, GROUP * P]).rearrange("p (k m) -> p k m", k=KH)
        xn = [carve([GROUP, D]).rearrange("p (b d) -> p b d", b=GROUP) for _ in range(2)]
        assert at <= NB * W2

        done1 = x1_at[NB - 1]
        l_ew = lane("l_ew")
        clear = [x1_at[loaded]]
        sp.dma(l_ew, r1, rw1.rearrange("(k p) n -> p k n", p=P), after=clear)
        sp.dma(l_ew, r2, rw2)
        sp.dma(l_ew, bias_rows[0:NE * KH, :], eb1.rearrange("e (k p) -> (e k) p", p=P))
        sp.dma(l_ew, bias_rows[NE * KH:2 * NE * KH, :], eb2.rearrange("e (k p) -> (e k) p", p=P))
        sp.dma(l_ew, bias_rows[2 * NE * KH:NBR, :], rb1.rearrange("(a n) -> a n", a=1))
        sp.dma(l_ew, row_b2, rb2.rearrange("(a n) -> a n", a=1))
        sp.dma(l_ew, row_b3, eb3)
        for k_out, a in ((e1, ew1), (e2, ew2), (e3, ew3)):
            got_ew = sp.dma(l_ew, k_out, a.rearrange("e (k p) n -> p e k n", p=P))
        t_bias = pe.put(lambda e: e.transpose(ps[7][:, 0:NBR], bias_rows, ident[0:NBR, 0:NBR]),
                        after=[got_ew, sums2])
        got_bias = act.put(lambda e: e.activation(bias_cols, ps[7][:, 0:NBR], ACT.Copy), after=[t_bias, done1])
        v_lpad = dve.put(lambda e: e.memset(logits, -1e30), after=[done1])

        groups = [range(g, min(g + GROUP, NB)) for g in range(0, NB, GROUP)]
        xn_at, turned, moved, rh_at, log_ps, gate_at, gate_read, pick_read, xnT_read, gts_read = ({} for _ in range(10))

        def scales(g):
            blocks = groups[g]
            b0, n = blocks[0], len(blocks)
            for b in blocks:
                v = dve.put(lambda e, b=b: e.bn_aggr(mv[:, b, :], stats[:, b, :]), after=[stat[b]])
            v_rstd = layer_norm_scales([v], b0, n)
            for i, b in enumerate(blocks):
                xn_at[g] = dve.put(lambda e, i=i, b=b: e.tensor_scalar(
                    xn[g % 2][:, i, :], node[:, b, :], mv[:, b, 0:1], rstd[:, b:b + 1], ALU.subtract, ALU.mult),
                    after=[v_rstd, done1] + ([turned[g - 2]] if g >= 2 else []))

        def turn(g):
            n = len(groups[g])
            for j in range(0, n, 2):
                bank, m = ps[6 + j // 2], min(2, n - j)
                clear = ([gate_at[g - 1]] if g else [got_bias]) if j == 0 else ([gts_read[g - 2]] if g >= 2 else [])
                for i in range(m):
                    for k in range(KD):
                        at = (i * KD + k) * P
                        turned[g] = pe.put(lambda e, i=i, j=j, k=k, at=at, bank=bank: e.transpose(
                            bank[:, at:at + P], xn[g % 2][:, j + i, k * P:(k + 1) * P], ident[:, :]),
                            after=[xn_at[g]] + clear)
                moved[g] = act.put(lambda e, j=j, m=m, bank=bank: e.activation(
                    xnT[g % 2][:, j:j + m, :, :].rearrange("p b k m -> p (b k m)"), bank[:, 0:m * D], ACT.Copy),
                    after=[turned[g], done1] + ([xnT_read[g - 2]] if g >= 2 else []))

        def route(g):
            n = len(groups[g])
            for k in range(KD):
                t = pe.put(lambda e, k=k: e.matmul(ps[7][:, 0:n * P], r1[:, k, :], xnT[g % 2][:, 0:n, k, :],
                                                   start=(k == 0), stop=(k == KD - 1)),
                           after=[moved[g], got_bias] + ([gts_read[g - 2]] if g >= 2 else []))
            rh_at[g] = act.put(lambda e: e.activation(rh[:, 0:n * P], ps[7][:, 0:n * P], ACT.Relu, bias=br1),
                               after=[t, done1, got_bias] + ([log_ps[g - 1]] if g else []))

        def choose(g):
            n = len(groups[g])
            for i in range(n):
                pe.put(lambda e, i=i: e.matmul(ps[6][:, i * TOP_PAD:i * TOP_PAD + NE], rh[:, i * P:(i + 1) * P], r2,
                                               start=True, stop=False), after=[rh_at[g], moved[g]])
                log_ps[g] = pe.put(lambda e, i=i: e.matmul(ps[6][:, i * TOP_PAD:i * TOP_PAD + NE], ones[0:1, :],
                                                           row_b2, start=False, stop=True))
            v = dve.put(lambda e: e.tensor_copy(
                logits[:, 0:n, 0:NE],
                ps[6][:, 0:n * TOP_PAD].rearrange("p (i m) -> p i m", m=TOP_PAD)[:, :, 0:NE]),
                after=[log_ps[g], v_lpad])
            top_u = top_i.bitcast(U32)
            for i in range(n):
                v_t = dve.put(lambda e, i=i: e.max(top[:, i, :], logits[:, i, :]), after=[v])
            for i in range(n):
                v_t = dve.put(lambda e, i=i: e.max_index(top_u[:, i, :], top[:, i, :], logits[:, i, :]), after=[v_t])
            shape = [P, n, TOP_PAD]
            pk, gt = pick[:, 0:n, :], gates[g % 2][:, 0:n, :]
            s_sum, s_p1, s_p2, s_w1, s_w2, s_d, s_i1, s_i2 = (scal[:, i, 0:n] for i in range(8))
            v = dve.put(lambda e: e.tensor_tensor(pk, logits[:, 0:n, :], top[:, 0:n, 0:1].to_broadcast(shape),
                                                  ALU.subtract), after=[v_t])
            a = act.put(lambda e: e.activation(pk, pk, ACT.Exp), after=[v])
            v = dve.put(lambda e: e.tensor_tensor(s_d, top[:, 0:n, 1], top[:, 0:n, 0], ALU.subtract))
            a2 = act.put(lambda e: e.activation(s_p2, s_d, ACT.Exp), after=[v])
            v = dve.put(lambda e: e.tensor_reduce(s_sum, pk[:, :, 0:NE], AX_X, ALU.add), after=[a])
            v = dve.put(lambda e: e.reciprocal(s_p1, s_sum), after=[v])
            v = dve.put(lambda e: e.tensor_tensor(s_p2, s_p2, s_p1, ALU.mult), after=[a2, v])
            v = dve.put(lambda e: e.tensor_tensor(s_d, s_p2, s_p1, ALU.subtract), after=[v])
            a = act.put(lambda e: e.activation(s_w2, s_d, ACT.Exp), after=[v])
            dve.put(lambda e: e.tensor_copy(s_i1, top_u[:, 0:n, 0]))
            v = dve.put(lambda e: e.tensor_copy(s_i2, top_u[:, 0:n, 1]))
            numbers = iota[:, 0:TOP_PAD].unsqueeze(1).to_broadcast(shape)
            dve.put(lambda e: e.tensor_tensor(gt, numbers, s_i1.unsqueeze(2).to_broadcast(shape), ALU.is_equal),
                    after=[v] + ([gate_read[g - 2]] if g >= 2 else []))
            v = dve.put(lambda e: e.tensor_tensor(pk, numbers, s_i2.unsqueeze(2).to_broadcast(shape), ALU.is_equal))
            v1 = dve.put(lambda e: e.tensor_scalar(s_w1, s_w2, 1.0, None, ALU.add), after=[a])
            v1 = dve.put(lambda e: e.reciprocal(s_w1, s_w1), after=[v1])
            v1 = dve.put(lambda e: e.tensor_tensor(s_w2, s_w2, s_w1, ALU.mult), after=[v1])
            dve.put(lambda e: e.tensor_tensor(gt, gt, s_w1.unsqueeze(2).to_broadcast(shape), ALU.mult))
            v = dve.put(lambda e: e.tensor_tensor(pk, pk, s_w2.unsqueeze(2).to_broadcast(shape), ALU.mult), after=[v1])
            gate_at[g] = dve.put(lambda e: e.tensor_tensor(gt, gt, pk, ALU.add), after=[v])

        l_out = lane("l_out")
        h1_at, h2_at, h1_read, y_at = {}, {}, {}, {}
        YS = 2
        n_y = 0
        y_read = {}

        def y_place(i):
            return ps[4 + i % YS][:, 0:D]

        def layer1(g, ex):
            n = len(groups[g])
            for m in range(KH):
                for k in range(KD):
                    t = pe.put(lambda e, m=m, k=k: e.matmul(
                        ps[m][:, 0:n * P], e1[:, ex, k, m * P:(m + 1) * P], xnT[g % 2][:, 0:n, k, :],
                        start=(k == 0), stop=(k == KD - 1)),
                        after=[moved[g], got_bias] + ([h1_at[m]] if m in h1_at else []))
                h1_at[m] = act.put(lambda e, m=m: e.activation(
                    h1[:, m, 0:n * P], ps[m][:, 0:n * P], ACT.Relu, bias=b1[:, ex, m:m + 1]),
                    after=[t, done1] + h1_read.get("all", []))
            xnT_read[g] = t

        def layer2(g, ex):
            n = len(groups[g])
            for m in range(KH):
                for k in range(KH):
                    t = pe.put(lambda e, m=m, k=k: e.matmul(
                        ps[2 + m][:, 0:n * P], e2[:, ex, k, m * P:(m + 1) * P], h1[:, k, 0:n * P],
                        start=(k == 0), stop=(k == KH - 1)),
                        after=[h1_at[k]] + ([h2_at[m]] if m in h2_at else []))
                h2_at[m] = act.put(lambda e, m=m: e.activation(
                    h2[:, m, 0:n * P], ps[2 + m][:, 0:n * P], ACT.Relu, bias=b2[:, ex, m:m + 1]),
                    after=[t, done1] + y_read.get("all", []))
            h1_read["all"] = [t]

        def layer3(g, ex):
            nonlocal n_y
            n = len(groups[g])
            for i, b in enumerate(groups[g]):
                for k in range(KH):
                    t = pe.put(lambda e, i=i, k=k, at=y_place(n_y): e.matmul(
                        at, h2[:, k, i * P:(i + 1) * P], e3[:, ex, k, :], start=(k == 0), stop=(k == KH - 1)),
                        after=[h2_at[k]] + ([y_at[n_y - YS]] if n_y >= YS else []))
                y_at[n_y] = dve.put(lambda e, i=i, b=b, at=y_place(n_y): e.scalar_tensor_tensor(
                    node[:, b, :], at, gates[g % 2][:, i, ex:ex + 1], node[:, b, :], ALU.mult, ALU.add),
                    after=[t, gate_at[g]] + ([y_at[n_y - n]] if n_y >= n else []))
                n_y += 1
            y_read["all"] = [t]

        def last_bias(g):
            nonlocal n_y
            n = len(groups[g])
            for i in range(n):
                t = pe.put(lambda e, i=i: e.transpose(ps[7][0:NE, i * P:(i + 1) * P], gates[g % 2][:, i, 0:NE],
                                                      ident[:, :]),
                           after=[gate_at[g], rh_at[min(g + 1, len(groups) - 1)]])
            gts_read[g] = act.put(lambda e: e.activation(gateT[0:NE, 0:n * P], ps[7][0:NE, 0:n * P], ACT.Copy),
                                  after=[t, done1] + y_read.get("bias", []))
            gate_read[g] = t
            for i, b in enumerate(groups[g]):
                t = pe.put(lambda e, i=i, at=y_place(n_y): e.matmul(at, gateT[0:NE, i * P:(i + 1) * P], row_b3,
                                                                    start=True, stop=True),
                           after=[gts_read[g], y_at[n_y - YS]])
                y_at[n_y] = dve.put(lambda e, b=b, at=y_place(n_y): e.tensor_tensor(
                    node[:, b, :], at, node[:, b, :], ALU.add), after=[t, y_at[n_y - n]])
                n_y += 1
            y_read["bias"] = [t]

        def store(g):
            blocks = groups[g]
            b0, n = blocks[0], len(blocks)
            full = n if blocks[-1] < NB - 1 else n - 1
            if full:
                done = sp.dma(l_out, out[b0 * P:(b0 + full) * P, :].rearrange("(b p) d -> p b d", p=P),
                              node[:, b0:b0 + full, :], after=[y_at[n_y - 1]])
            if full < n:
                done = sp.dma(l_out, out[(NB - 1) * P:N, :], node[0:LAST, NB - 1, :], after=[y_at[n_y - 1]])
            return done

        for step in (scales, turn, route, choose):
            step(0)
        layer1(0, 0)
        for g in range(len(groups)):
            for ex in range(NE):
                layer2(g, ex)
                if ex + 1 < NE:
                    layer1(g, ex + 1)
                elif g + 1 < len(groups):
                    layer1(g + 1, 0)
                layer3(g, ex)
                if g + 1 < len(groups) and ex < 4:
                    (scales, turn, route, choose)[ex](g + 1)
            last_bias(g)
            stored = store(g)
        for done in (stored, h_written, seg_out, list_zeroed, scattered):
            sp.wait(done)

        block = ctx.enter_context(nc.Block())

        @block.sync
        def _(e):
            sp.run(e)

        @block.tensor
        def _(e):
            pe.run(e)

        @block.vector
        def _(e):
            dve.run(e)

        @block.scalar
        def _(e):
            act.run(e)

        @block.gpsimd
        def _(e):
            pool.run(e)


_INS = ["x", "src", "dst", "L0_gnn_W_root", "L0_gnn_W_neigh", "L0_gnn_b", "L0_ffn_router_w1", "L0_ffn_router_b1",
        "L0_ffn_router_w2", "L0_ffn_router_b2", "L0_ffn_expert_w1", "L0_ffn_expert_b1", "L0_ffn_expert_w2",
        "L0_ffn_expert_b2", "L0_ffn_expert_w3", "L0_ffn_expert_b3"]


def kernel(**inputs):
    import numpy as np
    import concourse.bacc as bacc
    from concourse.bass_utils import run_bass_kernel_spmd

    nc = bacc.Bacc("TRN2", target_bir_lowering=False, num_devices=1)
    arrays, args = {}, []
    for name in _INS:
        a = np.ascontiguousarray(inputs[name])
        arrays[f"in_{name}"] = a
        args.append(nc.dram_tensor(f"in_{name}", a.shape, mybir.dt.from_np(a.dtype), kind="ExternalInput").ap())
    args.append(nc.dram_tensor("result", arrays["in_x"].shape, F32, kind="ExternalOutput").ap())
    gnn_moe_kernel(nc, *args)
    done = run_bass_kernel_spmd(nc, [arrays], core_ids=[0])
    return done.results[0]["result"]
```

```python
from contextlib import ExitStack

import concourse.bass as bass
from concourse import mybir

F32 = mybir.dt.float32
F16 = mybir.dt.float16
I32 = mybir.dt.int32
U32 = mybir.dt.uint32
ALU = mybir.AluOpType
ACT = mybir.ActivationFunctionType
AX_X = mybir.AxisListType.X

P = 128
EPS = 1e-5
SQUARES = 6
HOTS = 6
BANKS = 4
LAG = 3
TOP_PAD = 8
GROUP = 4


class Lane:

    def __init__(self, sem):
        self.sem, self.value = sem, 0

    def add(self, by):
        self.value += by
        return (self, self.value)


class Queue:

    def __init__(self, lane):
        self.steps, self.lane, self.seen = [], lane, {}

    def put(self, issue, after=(), lane=None, by=1):
        waits = []
        for other, value in after:
            if self.seen.get(id(other), 0) < value:
                self.seen[id(other)] = value
                waits.append((other.sem, value))
        lane = lane or self.lane
        self.steps.append((waits, issue, lane.sem, by))
        return lane.add(by)

    def dma(self, lane, out, in_, after=()):
        return self.put(lambda e: e.dma_start(out, in_), after, lane, 16)

    def prepare(self, issue, after=()):
        self.steps.append(([(other.sem, value) for other, value in after], issue, None, 0))

    def wait(self, event):
        self.steps.append(([(event[0].sem, event[1])], None, None, 0))

    def run(self, engine):
        for waits, issue, sem, by in self.steps:
            for other, value in waits:
                engine.wait_ge(other, value)
            if sem is not None:
                issue(engine).then_inc(sem, by)
            elif issue is not None:
                issue(engine)


def gnn_moe_kernel(nc, x, src, dst, w_root, w_neigh, b_gnn, rw1, rb1, rw2, rb2,
                   ew1, eb1, ew2, eb2, ew3, eb3, out):
    N, D = x.shape
    E = src.shape[0]
    NE, _, HID = ew1.shape
    RH = rw1.shape[1]
    KD = D // P
    KH = HID // P
    NB = -(-N // P)
    LAST = N - (NB - 1) * P
    FULL, TAIL = divmod(E, P)
    T = FULL + (TAIL > 0)
    C = 8
    TC = -(-T // C)
    TW = C * TC
    R8 = 8
    RT = P // R8
    GG = -(-((TC * P + NB * (R8 - 1)) // R8) // P)
    HI = GG * R8
    NT = ((E + C * NB * (R8 - 1)) // R8 + NB * (RT - 1)) // RT
    NTR = -(-NT // R8) * R8
    SPARE_ROW = NTR * RT
    TJ = -(-NT // P)
    W1 = D + 2
    W2 = 2 * D
    CODE = 256
    HALF = 1024

    with ExitStack() as ctx:
        def sb(name, shape, dt=F32):
            return ctx.enter_context(nc.sbuf_tensor(name, shape, dt))

        def lane(name):
            return Lane(ctx.enter_context(nc.semaphore(name)))

        xn_table = nc.dram_tensor("xn_table", [NB * P, D], F32, kind="Internal").ap()
        h_table = nc.dram_tensor("h_table", [NB * P, D], F32, kind="Internal").ap()
        edge_list = nc.dram_tensor("edge_list", [SPARE_ROW + C * GG * P, R8], F32, kind="Internal").ap()
        block_of = nc.dram_tensor("block_of", [1, P * TJ], I32, kind="Internal").ap()

        node = sb("node", [P, NB, D])
        big = sb("big", [P, NB * W2])
        rank = big[:, 0:NB * TW // 2].bitcast(F16).rearrange("p (b t) -> p b t", b=NB)
        acc = big[:, :]
        SLOTS = 24
        arena = sb("arena", [P, SLOTS * W1 + 2 * D])
        BT = 8
        assert TC % BT == 0
        src_i, dst_i = (arena[:, i * TW:(i + 1) * TW].bitcast(I32) for i in range(2))
        halves = arena[:, 2 * TW:4 * TW].bitcast(F16).rearrange("p (a t) -> p a t", a=4)
        high, low, lane_of, col_of = (halves[:, i, :] for i in range(4))
        sort_f = arena[:, 4 * TW:4 * TW + BT * (P + 2 * HI) + BT * HI // 2].bitcast(F16)
        hot_lane = sort_f[:, 0:2 * BT * P].rearrange("p (r m t) -> p r m t", r=2, t=BT)
        hot_col = sort_f[:, 2 * BT * P:2 * BT * (P + 2 * HI)].rearrange("p (r a m t) -> p r a m t", r=2, a=2, t=BT)
        is_col_a = sort_f[:, 2 * BT * (P + 2 * HI):].rearrange("p (m t) -> p m t", t=BT)
        free = node[:, :, :].rearrange("p b d -> p (b d)")
        taken = 0

        def take(n):
            nonlocal taken
            taken += n
            assert taken <= NB * D
            return free[:, taken - n:taken]

        bucket_i = take(TW).bitcast(I32)
        bucket_h = take(TW // 2).bitcast(F16)
        other_i = take(TW).bitcast(I32)
        HR = 3
        hot_h = [take(TW // 2).bitcast(F16) for _ in range(HR)]
        shifted = [take(TW) for _ in range(2)] + [arena[:, (4 + i) * TW:(5 + i) * TW] for i in range(3)]
        SR = len(shifted)
        term = [take(TW) for _ in range(HR)]

        def take_cb(n=NB):
            return take(C * n).rearrange("p (c b) -> p c b", c=C)

        upto, count, nrow, cum, row0, base, before, move = (take_cb() for _ in range(8))
        nrow_i = take(C * NB).bitcast(I32)
        row_at, jump = take_cb(NB + 1), take_cb(NB + 1)
        rows1 = arena[:, 0:SLOTS * W1].rearrange("p (r w) -> p r w", w=W1)
        rows2 = arena[:, 0:SLOTS * D].rearrange("p (r w) -> p r w", w=D)
        hot = sb("hot", [P, HOTS, P])
        iota = sb("iota", [P, P])
        ident = sb("ident", [P, P])
        below = sb("below", [P, P])
        ones = sb("ones", [P, P])
        idx = sb("idx", [P, NT], U32)
        local = sb("local", [P, NTR])
        iota_t = hot[:, :, :].rearrange("p r m -> p (r m)")[:, 0:P * BT // 2].bitcast(F16).rearrange(
            "p (m t) -> p m t", t=BT)
        rownum = sb("rownum", [P, GG])
        small = sb("small", [P, 8, NB])
        small_i = sb("small_i", [P, 2, NB], I32)
        seg = sb("seg", [P, TJ])
        seg_k = sb("seg_k", [P, TJ])
        seg_i = sb("seg_i", [P, TJ], I32)
        offs = sb("offs", [1, P * TJ], I32)
        stats = sb("stats", [P, NB, 6])
        mv = sb("mv", [P, NB, 2])
        rstd = sb("rstd", [P, NB])
        nsc = sb("nsc", [P, 3, NB])
        deg = sb("deg", [P, NB])
        rden = sb("rden", [P, NB])
        wg = sb("wg", [P, 2 * KD, D])
        bg = sb("bg", [1, D])
        tmp = sb("tmp", [P, 2, 2 * D])
        lhs = sb("lhs", [P, 2, 2 * KD * P])

        ps = [ctx.enter_context(nc.psum_tensor(f"ps{i}", [P, 512], F32)) for i in range(8)]

        pe, dve, act, pool, sp = (Queue(lane(f"s_{n}")) for n in ("pe", "dve", "act", "pool", "sp"))

        m_src = dve.put(lambda e: e.memset(src_i[:, FULL:TW], NB * P))
        m_dst = dve.put(lambda e: e.memset(dst_i[:, FULL:TW], 0))
        l_edges = lane("l_edges")
        for t, a in ((src_i, src), (dst_i, dst)):
            got_edges = sp.dma(l_edges, t[:, 0:FULL], a[0:P * FULL].rearrange("(p t) -> p t", p=P))
            if TAIL:
                got_edges = sp.dma(l_edges, t[0:TAIL, FULL:T], a[P * FULL:E].rearrange("(p t) -> p t", t=1),
                                   after=[m_src, m_dst])
        l_w = lane("l_w")
        sp.dma(l_w, wg[:, 0:KD, :], w_root.rearrange("(k p) n -> p k n", p=P))
        sp.dma(l_w, wg[:, KD:2 * KD, :], w_neigh.rearrange("(k p) n -> p k n", p=P))
        got_wg = sp.dma(l_w, bg[:, :], b_gnn.rearrange("(a n) -> a n", a=1))

        c_iota = pool.put(lambda e: e.iota(iota[:, :], [[1, P]], base=0, channel_multiplier=0,
                                           allow_small_or_imprecise_dtypes=True))
        c_segk = pool.put(lambda e: e.iota(seg_k[:, :], [[1, TJ]], base=0, channel_multiplier=TJ,
                                           allow_small_or_imprecise_dtypes=True))
        c_row = pool.put(lambda e: e.iota(rownum[:, :], [[P, GG]], base=0, channel_multiplier=1,
                                          allow_small_or_imprecise_dtypes=True))
        c_ones = pool.put(lambda e: e.memset(ones[:, :], 1.0))
        c_zero = pool.put(lambda e: e.memset(local[:, :], 0.0))
        z_id = pool.put(lambda e: e.memset(ident[:, :], 0.0))
        c_id = pool.put(lambda e: e.affine_select(out=ident[:, :], in_=ident[:, :], compare_op=ALU.not_equal,
                                                  fill=1.0, base=0, pattern=[[-1, P]], channel_multiplier=1),
                        after=[z_id])
        c_below = pool.put(lambda e: e.affine_select(out=below[:, :], in_=ones[:, :], compare_op=ALU.is_ge,
                                                     fill=0.0, base=-1, pattern=[[1, P]],
                                                     channel_multiplier=-1), after=[c_ones])
        l_zero = lane("l_zero")
        list_rows = edge_list[0:SPARE_ROW, :].rearrange("(p k) a -> p (k a)", p=P)
        list_zeroed = sp.dma(l_zero, list_rows, local[:, :], after=[c_zero])

        v_ih = dve.put(lambda e: e.tensor_copy(iota_t, iota[:, :].unsqueeze(2).to_broadcast([P, P, BT])),
                       after=[c_iota])
        v_bi = dve.put(lambda e: e.tensor_scalar(bucket_i, src_i, 7, None, ALU.logical_shift_right),
                       after=[got_edges])
        v_bh = dve.put(lambda e: e.tensor_copy(bucket_h, bucket_i), after=[v_bi])
        v_hot, v_scan = {}, {}
        for b in range(NB + 1):
            if b < NB:
                v_hot[b] = dve.put(lambda e, b=b: e.tensor_scalar(hot_h[b % HR], bucket_h, float(b), None,
                                                                  ALU.is_equal),
                                   after=[v_bh] + ([v_scan[b - HR]] if b >= HR else []))
            if b:
                v_scan[b - 1] = dve.put(lambda e, b=b - 1: e.tensor_tensor_scan(
                    rank[:, b, :], hot_h[b % HR], hot_h[b % HR], 0.0, ALU.add, ALU.bypass), after=[v_hot[b - 1]])

        v = dve.put(lambda e: e.tensor_copy(upto, rank[:, :, TC - 1:TW:TC].rearrange("p b c -> p c b")),
                    after=[v_scan[NB - 1]])
        v = dve.put(lambda e: e.tensor_copy(count[:, 0, :], upto[:, 0, :]), after=[v])
        v_cnt = dve.put(lambda e: e.tensor_tensor(count[:, 1:C, :], upto[:, 1:C, :], upto[:, 0:C - 1, :],
                                                  ALU.subtract), after=[v])

        def flat(a):
            return a.rearrange("p c b -> p (c b)")

        pe.put(lambda e: e.matmul(ps[0][:, 0:C * NB], below[:, :], flat(count), start=True, stop=True),
               after=[v_cnt, c_below])
        t_tot = pe.put(lambda e: e.matmul(ps[1][:, 0:C * NB], ones[:, :], flat(count), start=True, stop=True))
        v = dve.put(lambda e: e.tensor_scalar(nrow_i, ps[1][:, 0:C * NB], float(R8 - 1), None, ALU.add),
                    after=[t_tot])
        v = dve.put(lambda e: e.tensor_scalar(nrow_i, nrow_i, 3, None, ALU.logical_shift_right), after=[v])
        v_nr = dve.put(lambda e: e.tensor_copy(flat(nrow), nrow_i), after=[v])
        v = dve.put(lambda e: e.tensor_tensor_scan(flat(cum), flat(nrow), flat(nrow), 0.0, ALU.add, ALU.bypass),
                    after=[v_nr])
        v = dve.put(lambda e: e.tensor_tensor(row0, cum, nrow, ALU.subtract), after=[v])
        v_r0 = dve.put(lambda e: e.tensor_tensor(row0[:, 1:C, :], row0[:, 1:C, :],
                                                 cum[:, 0:C - 1, NB - 1:NB].to_broadcast([P, C - 1, NB]),
                                                 ALU.subtract), after=[v])
        v = dve.put(lambda e: e.tensor_scalar(base, row0, float(R8), -1.0, ALU.mult, ALU.add), after=[v_r0])
        v = dve.put(lambda e: e.tensor_tensor(flat(base), flat(base), ps[0][:, 0:C * NB], ALU.add), after=[v])
        v = dve.put(lambda e: e.tensor_tensor(base, base, upto, ALU.subtract), after=[v])
        v_base = dve.put(lambda e: e.tensor_tensor(base, base, count, ALU.add), after=[v])

        v_shift, v_picks, v_term, t_place = {}, {}, {}, {}

        def pick_block(b):
            v_term[b] = dve.put(lambda e: e.tensor_tensor(term[b % HR], shifted[b % SR], hot_h[b % HR], ALU.mult),
                                after=[v_picks[b], v_shift[b]] + ([t_place[b - HR]] if b >= HR else []))
            for i in range(2):
                t_place[b] = pe.put(lambda e, i=i: e.matmul(
                    ps[2 + i][:, 0:TW // 2], ident[:, :], term[b % HR][:, i * TW // 2:(i + 1) * TW // 2],
                    start=(b == 0), stop=(b == NB - 1)), after=[v_term[b], c_id])

        for b in range(NB):
            free = [v_term[b - SR]] if b >= SR else [v_bh]
            if b % 2:
                v_shift[b] = pool.put(lambda e, b=b: e.tensor_tensor(
                    shifted[b % SR].rearrange("p (c t) -> p c t", c=C),
                    rank[:, b, :].rearrange("p (c t) -> p c t", c=C),
                    base[:, :, b:b + 1].to_broadcast([P, C, TC]), ALU.add), after=[v_base] + free)
            else:
                for c in range(C):
                    v_shift[b] = act.put(lambda e, b=b, c=c: e.activation(
                        shifted[b % SR][:, c * TC:(c + 1) * TC], rank[:, b, c * TC:(c + 1) * TC], ACT.Identity,
                        bias=base[:, c, b:b + 1]), after=[v_base] + free)
            v_picks[b] = dve.put(lambda e, b=b: e.tensor_scalar(hot_h[b % HR], bucket_h, float(b), None, ALU.is_equal),
                                 after=[v_scan[NB - 1]] + ([v_term[b - HR]] if b >= HR else []))
            if b:
                pick_block(b - 1)
        pick_block(NB - 1)

        v = dve.put(lambda e: e.tensor_scalar(bucket_i, dst_i, 2, None, ALU.logical_shift_right), after=[v_bh])
        v = dve.put(lambda e: e.tensor_copy(high, bucket_i), after=[v])
        v = dve.put(lambda e: e.tensor_scalar(bucket_i, dst_i, 3, 8, ALU.bitwise_and, ALU.logical_shift_left),
                    after=[v])
        v = dve.put(lambda e: e.tensor_scalar(other_i, src_i, P - 1, None, ALU.bitwise_and), after=[v])
        v = dve.put(lambda e: e.memset(low[:, FULL:TW], 0.0), after=[v])
        for rows_, a, z in ((P, 0, FULL), (TAIL, FULL, T)):
            if rows_ and z > a:
                v_low = dve.put(lambda e, n=rows_, a=a, z=z: e.scalar_tensor_tensor(
                    low[0:n, a:z], bucket_i[0:n, a:z], 1.0, other_i[0:n, a:z], ALU.add, ALU.add), after=[v])
        slot_i, low3 = bucket_i, other_i
        for i in range(2):
            v = dve.put(lambda e, i=i: e.tensor_copy(slot_i[:, i * TW // 2:(i + 1) * TW // 2], ps[2 + i][:, 0:TW // 2]),
                        after=[t_place[NB - 1], v_low])
        lane_i = shifted[0].bitcast(I32)
        dve.put(lambda e: e.tensor_scalar(lane_i, slot_i, 3, P - 1, ALU.logical_shift_right, ALU.bitwise_and),
                after=[v])
        v = dve.put(lambda e: e.tensor_scalar(low3, slot_i, R8 - 1, None, ALU.bitwise_and))
        v = dve.put(lambda e: e.tensor_scalar(slot_i, slot_i, 10, 3, ALU.logical_shift_right,
                                              ALU.logical_shift_left), after=[v])
        dve.put(lambda e: e.tensor_copy(lane_of, lane_i), after=[v])
        v_col = dve.put(lambda e: e.tensor_tensor(col_of, slot_i, low3, ALU.add), after=[v])

        rows_b, nt_f, end_f, start_f = (small[:, i, :] for i in range(4))
        v = dve.put(lambda e: e.memset(before[:, 0, :], 0.0), after=[v_nr])
        for c in range(1, C):
            v = dve.put(lambda e, c=c: e.tensor_tensor(before[:, c, :], before[:, c - 1, :], nrow[:, c - 1, :],
                                                       ALU.add), after=[v])
        v = dve.put(lambda e: e.tensor_tensor(rows_b, before[:, C - 1, :], nrow[:, C - 1, :], ALU.add), after=[v])
        v = dve.put(lambda e: e.tensor_scalar(small_i[:, 0, :], rows_b, float(RT - 1), None, ALU.add), after=[v])
        v = dve.put(lambda e: e.tensor_scalar(small_i[:, 1, :], small_i[:, 0, :], 4, None, ALU.logical_shift_right),
                    after=[v])
        v = dve.put(lambda e: e.tensor_copy(nt_f, small_i[:, 1, :]), after=[v])
        v_end = dve.put(lambda e: e.tensor_tensor_scan(end_f, nt_f, nt_f, 0.0, ALU.add, ALU.bypass), after=[v])
        v = dve.put(lambda e: e.tensor_tensor(start_f, end_f, nt_f, ALU.subtract), after=[v_end])
        v = dve.put(lambda e: e.tensor_scalar(start_f, start_f, float(RT), None, ALU.mult), after=[v])
        v = dve.put(lambda e: e.tensor_tensor(move, before, start_f.unsqueeze(1).to_broadcast([P, C, NB]), ALU.add),
                    after=[v])
        v_mv = dve.put(lambda e: e.tensor_tensor(move, move, row0, ALU.subtract), after=[v, v_r0])
        dve.put(lambda e: e.tensor_copy(row_at[:, :, 0:NB], row0))
        dve.put(lambda e: e.tensor_tensor(row_at[:, :, NB:NB + 1], row0[:, :, NB - 1:NB], nrow[:, :, NB - 1:NB],
                                          ALU.add))
        v = dve.put(lambda e: e.tensor_copy(jump[:, :, 0:1], move[:, :, 0:1]), after=[v_mv])
        v = dve.put(lambda e: e.tensor_tensor(jump[:, :, 1:NB], move[:, :, 1:NB], move[:, :, 0:NB - 1], ALU.subtract),
                    after=[v])
        for c in range(C):
            v_plan = dve.put(lambda e, c=c: e.tensor_scalar(
                jump[:, c, NB:NB + 1], move[:, c, NB - 1:NB], -1.0, float(SPARE_ROW + c * GG * P),
                ALU.mult, ALU.add), after=[v])

        at = 0

        def carve(n):
            nonlocal at
            at += n
            return big[:, at - n:at]

        lists = carve(C * HI).rearrange("p (c h) -> p c h", c=C)
        lowpart = carve(2 * HI).rearrange("p (c h) -> p c h", c=2)
        dest_f = carve(C * GG).rearrange("p (c g) -> p c g", c=C)
        dest = carve(C * GG).bitcast(U32).rearrange("p (c g) -> p c g", c=C)
        passed = [carve(GG * (NB + 1)).rearrange("p (g b) -> p g b", g=GG) for _ in range(2)]
        loaded_tiles = carve(TJ * P).rearrange("p (j q) -> p j q", j=TJ)
        code_f = carve(TW)
        is_col_b = carve(BT * HI // 2).bitcast(F16).rearrange("p (m t) -> p m t", t=BT)
        sorting_end = at
        cleared = {}

        def clear_piece(c):
            a, z = (sorting_end + (NB * W2 - sorting_end) * i // C for i in (c, c + 1))
            cleared[c] = pool.put(lambda e: e.memset(acc[:, a:z], 0.0), after=[t_place[NB - 1]])

        def list_rows_of(c):
            shape = [P, GG, NB + 1]
            a = passed[c % 2]
            v = dve.put(lambda e: e.tensor_tensor(a, row_at[:, c, :].unsqueeze(1).to_broadcast(shape),
                                                  rownum[:, :].unsqueeze(2).to_broadcast(shape), ALU.is_le),
                        after=[v_plan, c_row, t_place[NB - 1]])
            v = dve.put(lambda e: e.tensor_tensor(a, a, jump[:, c, :].unsqueeze(1).to_broadcast(shape), ALU.mult),
                        after=[v])
            v = dve.put(lambda e: e.tensor_reduce(dest_f[:, c, :], a, AX_X, ALU.add), after=[v])
            return dve.put(lambda e: e.tensor_tensor(dest[:, c, :], dest_f[:, c, :], rownum[:, :], ALU.add), after=[v])

        l_scatter = lane("l_scatter")
        t_sort, v_list, v_dest = {}, {}, {}

        def send_chunk(c):
            nonlocal scattered
            full = ps[4 + c % 2]
            a = act.put(lambda e: e.activation(lowpart[:, c % 2, :], full[:, HI:2 * HI], ACT.Copy),
                        after=[t_sort[(c + 1) * TC // BT - 1]] + ([v_list[c - 2]] if c >= 2 else [t_place[NB - 1]]))
            v_list[c] = dve.put(lambda e: e.scalar_tensor_tensor(lists[:, c, :], full[:, 0:HI], float(HALF),
                                                                 lowpart[:, c % 2, :], ALU.mult, ALU.add), after=[a])
            for g in range(GG):
                scattered = pool.put(lambda e, g=g: e.indirect_dma_start(
                    out=edge_list, out_offset=bass.IndirectOffsetOnAxis(ap=dest[:, c, g:g + 1], axis=0),
                    in_=lists[:, c, g * R8:(g + 1) * R8], in_offset=None),
                    after=[v_dest[c], v_list[c], list_zeroed], lane=l_scatter, by=16)
            if c < C - 1:
                clear_piece(c + 1)

        scattered = None
        col_read = {}
        BY_ACT = 6
        v_code = dve.put(lambda e: e.tensor_copy(code_f, high), after=[v_col, t_place[NB - 1]])
        clear_piece(0)
        for k in range(TW // BT):
            c, t = divmod(k, TC // BT)
            cols, r = slice(k * BT, (k + 1) * BT), k % 2
            old = [t_sort[k - 2]] if k >= 2 else []

            def across(a, m, cols=cols):
                return a[:, cols].unsqueeze(1).to_broadcast([P, m, BT])
            is_col = (is_col_a, is_col_b)[r]
            v_c = dve.put(lambda e, a=across(col_of, HI), is_col=is_col: e.tensor_tensor(
                is_col, iota_t[:, 0:HI, :], a, ALU.is_equal), after=[v_ih, v_col] + col_read.get(k - 2, []))
            v_hot = dve.put(lambda e, r=r, a=across(lane_of, P): e.tensor_tensor(
                hot_lane[:, r, :, :], iota_t, a, ALU.is_equal), after=old)
            made = [v_hot]
            for u in range(BY_ACT):
                a_ = act.put(lambda e, r=r, u=u, cols=cols, is_col=is_col: e.activation(
                    hot_col[:, r, 0, :, u], is_col[:, :, u], ACT.Copy,
                    scale=code_f[:, cols.start + u:cols.start + u + 1]), after=[v_c, v_code] + old)
            made.append(a_)
            for i, part, u in ((0, high, BY_ACT), (1, low, 0)):
                made.append(dve.put(lambda e, r=r, i=i, u=u, a=across(part, HI), is_col=is_col: e.tensor_tensor(
                    hot_col[:, r, i, :, u:BT], is_col[:, :, u:BT], a[:, :, u:BT], ALU.mult), after=[v_c] + old))
            col_read[k] = made[1:]
            for u in range(BT):
                first, last = t == 0 and u == 0, t == TC // BT - 1 and u == BT - 1
                t_sort[k] = pe.put(lambda e, c=c, r=r, u=u, first=first, last=last:
                                   e.matmul(ps[4 + c % 2][:, 0:2 * HI], hot_lane[:, r, :, u],
                                            hot_col[:, r, :, :, u].rearrange("p a m -> p (a m)"), start=first, stop=last),
                                   after=made + ([v_list[c - 2]] if c >= 2 else []))
            if t == 1 and c:
                send_chunk(c - 1)
            if k == 2:
                for c_ in range(C):
                    v_dest[c_] = list_rows_of(c_)
                z_node = dve.put(lambda e: e.memset(node[:, NB - 1, :], 0.0), after=[v_dest[C - 1]])
                l_x = lane("l_x")
                sp.dma(l_x, node[:, 0:NB - 1, :], x[0:(NB - 1) * P, :].rearrange("(b p) d -> p b d", p=P),
                       after=[z_node, t_place[NB - 1]])
                got_x = sp.dma(l_x, node[0:LAST, NB - 1, :], x[(NB - 1) * P:N, :])
        send_chunk(C - 1)
        v_place = v_list[C - 1]

        assert TJ * NB <= 4 * D
        seen = tmp[:, :, :].rearrange("p a n -> p (a n)")[:, 0:TJ * NB].rearrange("p (j b) -> p j b", b=NB)
        v = dve.put(lambda e: e.tensor_tensor(seen, end_f.unsqueeze(1).to_broadcast([P, TJ, NB]),
                                              seg_k[:, :].unsqueeze(2).to_broadcast([P, TJ, NB]), ALU.is_le),
                    after=[v_end, c_segk])
        v = dve.put(lambda e: e.tensor_reduce(seg[:, :], seen, AX_X, ALU.add), after=[v])
        v = dve.put(lambda e: e.tensor_scalar(seg[:, :], seg[:, :], float(NB - 1), None, ALU.min), after=[v])
        v_seg = dve.put(lambda e: e.tensor_scalar(seg_i[:, :], seg[:, :], float(W2), None, ALU.mult), after=[v])
        l_seg = lane("l_seg")
        seg_out = sp.dma(l_seg, block_of.rearrange("a (p j) -> p (a j)", p=P), seg_i[:, :], after=[v_seg])
        got_offs = sp.dma(l_seg, offs[:, :], block_of, after=[seg_out])

        def layer_norm_steps(stat_events, b0=0, n=NB):
            var, root, quot = (nsc[:, i, b0:b0 + n] for i in range(3))
            v0 = dve.put(lambda e: e.tensor_scalar(var, mv[:, b0:b0 + n, 1], EPS, None, ALU.add), after=stat_events)
            a0 = act.put(lambda e: e.activation(root, var, ACT.Sqrt), after=[v0])
            yield a0
            v1 = dve.put(lambda e: e.reciprocal(quot, root), after=[a0])
            v1 = dve.put(lambda e: e.tensor_tensor(quot, quot, var, ALU.mult), after=[v1])
            v1 = dve.put(lambda e: e.tensor_tensor(root, root, quot, ALU.add), after=[v1])
            v1 = dve.put(lambda e: e.tensor_scalar(root, root, 0.5, None, ALU.mult), after=[v1])
            yield dve.put(lambda e: e.reciprocal(rstd[:, b0:b0 + n], root), after=[v1])

        stat = [dve.put(lambda e, b=b: e.bn_stats(stats[:, b, :], node[:, b, :]), after=[got_x]) for b in range(NB)]
        v = [dve.put(lambda e, b=b: e.bn_aggr(mv[:, b, :], stats[:, b, :]), after=[stat[b]]) for b in range(NB)]
        _, v_rstd = layer_norm_steps(v)
        l_tab = lane("l_tab")
        CH = 7
        xn_at = {}

        def root_product(b):
            for j in range(KD):
                pe.put(lambda e, b=b, j=j: e.matmul(ps[6 + b % 2][:, 0:D], lhs[:, b % 2, j * P:(j + 1) * P],
                                                    wg[:, j, :], start=(j == 0), stop=False),
                       after=[moved[b], got_wg] + ([r_at[b - 2]] if b >= 2 else []))
            prod[b] = pe.put(lambda e, b=b: e.matmul(ps[6 + b % 2][:, 0:D], ones[0:1, :], bg[:, :],
                                                     start=False, stop=True))
            r_at[b] = act.put(lambda e, b=b: e.activation(node[:, b, :], ps[6 + b % 2][:, 0:D], ACT.Copy),
                              after=[prod[b], xn_written])

        for b in range(NB):
            xn_at[b] = v_xn = dve.put(lambda e, b=b: e.tensor_scalar(
                node[:, b, :], node[:, b, :], mv[:, b, 0:1], rstd[:, b:b + 1], ALU.subtract, ALU.mult), after=[v_rstd])
            if b % CH == CH - 1 or b == NB - 1:
                b0 = b - b % CH
                xn_written = sp.dma(l_tab, xn_table[b0 * P:(b + 1) * P, :].rearrange("(b p) d -> p b d", p=P),
                                    node[:, b0:b + 1, :], after=[v_xn])

        turned, moved, prod, r_at = {}, {}, {}, {}

        def root_block(b):
            if b < NB:
                for j in range(KD):
                    turned[b] = pe.put(lambda e, j=j: e.transpose(ps[4 + b % 2][:, j * P:(j + 1) * P],
                                                                  node[:, b, j * P:(j + 1) * P], ident[:, :]),
                                       after=[xn_at[b], c_id] + ([moved[b - 2]] if b >= 2 else []))
                moved[b] = act.put(lambda e: e.activation(lhs[:, b % 2, 0:D], ps[4 + b % 2][:, 0:D], ACT.Copy),
                                   after=[turned[b]] + ([prod[b - 2]] if b >= 2 else []))
            if b:
                root_product(b - 1)

        l_list = lane("l_list")
        whole, rest = divmod(NT, P)
        tiles_of = edge_list[0:NT * RT, :].rearrange("(k u) e -> k (u e)", u=RT)
        listed = sp.dma(l_list, loaded_tiles[:, 0:whole, :],
                        tiles_of[0:whole * P, :].rearrange("(j p) q -> p j q", p=P), after=[scattered, v_dest[C - 1]])
        if rest:
            listed = sp.dma(l_list, loaded_tiles[0:rest, whole, :], tiles_of[whole * P:NT, :])
        per = 512 // P
        for j in range(TJ):
            n = min(P, NT - j * P)
            t_list = pe.put(lambda e, j=j, n=n: e.transpose(
                ps[j // per][:, (j % per) * P:(j % per) * P + n], loaded_tiles[0:n, j, :], ident[0:n, 0:n]),
                after=[listed, v_place])
        ci = arena[:, 0:NT].bitcast(I32)
        cl = arena[:, NT:2 * NT].bitcast(I32)
        for i in range(-(-TJ // per)):
            a, z = i * 512, min(NT, (i + 1) * 512)
            v = dve.put(lambda e, i=i, a=a, z=z: e.tensor_copy(ci[:, a:z], ps[i][:, 0:z - a]),
                        after=[t_list, t_sort[TW // BT - 1]])
        dve.put(lambda e: e.tensor_scalar(cl, ci, CODE - 1, None, ALU.bitwise_and), after=[v])
        v_idx = dve.put(lambda e: e.tensor_scalar(idx[:, :], ci.bitcast(U32), 8, None, ALU.logical_shift_right))
        v_local = dve.put(lambda e: e.tensor_scalar(local[:, 0:NT], cl, -1.0, None, ALU.add), after=[v_idx])

        l_row = [lane(f"l_row{i}") for i in range(SLOTS)]

        def edge_pass(table, table_written, width, first, cleared, square, beside=None):
            ring = SLOTS - SQUARES if square else SLOTS
            hot_at, got, squared, summed, added, place_of = {}, {}, {}, {}, {}, {}

            def load_offset(k):
                def issue(e):
                    place_of[k] = nc.values_load(
                        offs[0:1, k:k + 1], engines=[mybir.EngineType.DVE], min_val=0, max_val=(NB - 1) * W2,
                        skip_runtime_bounds_check_because="the block's number was limited to NB - 1")
                dve.prepare(issue, after=[got_offs] if k == 0 else [])

            def add(k):
                def issue(e):
                    block = acc[:, bass.ds(place_of[k], width)]
                    return e.tensor_tensor(block, ps[k % BANKS][:, 0:width], block, ALU.add)
                added[k] = dve.put(issue, after=[summed[k]] + ([added[k - 1]] if k else cleared))

            for k in range(NT + LAG):
                if LAG <= k:
                    load_offset(k - LAG)
                if k < NT:
                    def free(depth):
                        return [summed[k - depth]] if k >= depth else list(first)
                    slot, sq = k % ring, ring + k % SQUARES
                    row = rows2[:, slot, :] if square else rows1[:, slot, 0:D]
                    got[k] = pool.put(lambda e, k=k, row=row: e.indirect_dma_start(
                        out=row, out_offset=None, in_=table,
                        in_offset=bass.IndirectOffsetOnAxis(ap=idx[:, k:k + 1], axis=0)),
                        after=[v_idx, table_written] + free(ring), lane=l_row[slot], by=16)
                    hot_at[k] = dve.put(lambda e, k=k: e.tensor_scalar(
                        hot[:, k % HOTS, :], iota[:, :], local[:, k:k + 1], None, ALU.is_equal),
                        after=[v_local, c_iota] + free(HOTS))
                    need = [got[k], hot_at[k]]
                    moving, total = rows1[:, slot, :], ps[k % BANKS][:, 0:width]
                    if square:
                        squared[k] = act.put(lambda e, row=row, sq=sq: e.activation(rows2[:, sq, :], row, ACT.Square),
                                             after=[got[k]] + free(SQUARES))
                        need.append(squared[k])
                        moving = rows2[:, slot:sq + 1:sq - slot, :]
                        total = total.rearrange("p (a w) -> p a w", a=2)
                    need += [added[k - BANKS]] if k >= BANKS else list(first)
                    summed[k] = pe.put(lambda e, k=k, moving=moving, total=total: e.matmul(
                        total, hot[:, k % HOTS, :], moving, start=True, stop=True), after=need)
                if k >= LAG:
                    add(k - LAG)
                if beside and k % (NT // (NB + 2)) == 0 and k // (NT // (NB + 2)) <= NB:
                    beside(k // (NT // (NB + 2)))
            return added[NT - 1]

        v_one = dve.put(lambda e: e.memset(rows1[:, :, D:W1], 1.0), after=[v_local])
        v_clear = dve.put(lambda e: e.memset(acc[:, 0:sorting_end], 0.0), after=[v_local, scattered])
        sums1 = edge_pass(xn_table, xn_written, W1, [v_one], [v_clear, cleared[C - 1]], False, root_block)

        by_block = acc.rearrange("p (b w) -> p b w", w=W2)
        v_deg = dve.put(lambda e: e.tensor_copy(deg[:, :], by_block[:, :, D]), after=[sums1])
        v = dve.put(lambda e: e.tensor_scalar(rden[:, :], deg[:, :], 1.0, None, ALU.max), after=[v_deg])
        v_rden = dve.put(lambda e: e.reciprocal(rden[:, :], rden[:, :]), after=[v])
        turned, moved, prod, h_at, v_mean, h_written = {}, {}, {}, {}, {}, None
        HD = 3
        mean = arena[:, 0:HD * D].rearrange("p (r d) -> p r d", d=D)
        left = arena[:, HD * D:2 * HD * D].rearrange("p (r d) -> p r d", d=D)
        pre = arena[:, 2 * HD * D:3 * HD * D].rearrange("p (r d) -> p r d", d=D)

        def neighbour_product(b):
            nonlocal h_written
            for j in range(KD):
                prod[b] = pe.put(lambda e, b=b, j=j: e.matmul(
                    ps[HD + b % HD][:, 0:D], left[:, b % HD, j * P:(j + 1) * P], wg[:, KD + j, :],
                    start=(j == 0), stop=(j == KD - 1)), after=[moved[b]] + ([h_at[b - HD]] if b >= HD else []))
            v_pre = dve.put(lambda e, b=b: e.tensor_tensor(pre[:, b % HD, :], ps[HD + b % HD][:, 0:D],
                                                           node[:, b, :], ALU.add),
                            after=[prod[b], r_at[NB - 1]] + ([h_at[b - HD]] if b >= HD else []))
            h_at[b] = act.put(lambda e, b=b: e.activation(node[:, b, :], pre[:, b % HD, :], ACT.Relu),
                              after=[v_pre])
            if b % CH == CH - 1 or b == NB - 1:
                b0 = b - b % CH
                h_written = sp.dma(l_tab, h_table[b0 * P:(b + 1) * P, :].rearrange("(b p) d -> p b d", p=P),
                                   node[:, b0:b + 1, :], after=[h_at[b], xn_written])

        def mean_of(b):
            v_mean[b] = dve.put(lambda e: e.tensor_scalar(
                mean[:, b % HD, :], by_block[:, b, 0:D], rden[:, b:b + 1], None, ALU.mult),
                after=[v_rden] + ([turned[b - HD]] if b >= HD else []))
            cleared[b] = pool.put(lambda e: e.memset(by_block[:, b, :], 0.0), after=[v_mean[b], v_deg])

        cleared = {}

        mean_of(0)
        for b in range(NB + 1):
            if b + 1 < NB:
                mean_of(b + 1)
            if b < NB:
                for j in range(KD):
                    turned[b] = pe.put(lambda e, b=b, j=j: e.transpose(
                        ps[b % HD][:, j * P:(j + 1) * P], mean[:, b % HD, j * P:(j + 1) * P], ident[:, :]),
                        after=[v_mean[b]] + ([moved[b - HD]] if b >= HD else [sums1]))
                moved[b] = act.put(lambda e, b=b: e.activation(left[:, b % HD, :], ps[b % HD][:, 0:D], ACT.Copy),
                                   after=[turned[b], sums1] + ([prod[b - HD]] if b >= HD else []))
            if b:
                neighbour_product(b - 1)

        sums2 = edge_pass(h_table, h_written, W2, [h_at[NB - 1], prod[NB - 1]], [cleared[NB - 1]], True)

        groups = [range(g, min(g + GROUP, NB)) for g in range(0, NB, GROUP)]
        cut = [0, 5, 10, len(groups)]
        chunks = [range(groups[i][0], groups[j - 1][-1] + 1) for i, j in zip(cut, cut[1:])]
        tiles_in = [(2 * P * len(c) + NE * (P - 1)) // P for c in chunks]
        tile0 = [sum(tiles_in[:s]) for s in range(len(chunks) + 1)]
        XT = tile0[-1]
        CB, CT = max(len(c) for c in chunks), max(tiles_in)
        assert CT <= P
        W12 = KD * HID + KH * HID + 2 * KH
        REC = W12 + KH * D + D
        at = 0

        def carve(*shape, dt=F32):
            nonlocal at
            n = 1
            for d in shape:
                n *= d
            at += n
            piece = big[:, at - n:at]
            if dt != F32:
                piece = piece.bitcast(dt)
            if len(shape) == 2:
                piece = piece.rearrange("p (a b) -> p a b", a=shape[0])
            if len(shape) == 3:
                piece = piece.rearrange("p (a b c) -> p a b c", a=shape[0], b=shape[1])
            return piece

        r1 = carve(KD, RH)
        r2 = carve(NE)
        NBR = 2 * NE * KH + 1
        bias_rows = carve(P)[0:NBR, :]
        row_b2 = carve(NE)[0:1, :]
        bias_cols = carve(NBR)
        br1 = bias_cols[:, 2 * NE * KH:NBR]
        xn = [carve(GROUP, D) for _ in range(2)]
        xnT = [carve(GROUP, KD, P) for _ in range(2)]
        rh = carve(GROUP * P)
        logits = carve(NB, TOP_PAD)
        gate = carve(2, NB)
        y_row = carve(2, NB, dt=U32)
        shift = carve(NB)
        lane_no = carve(1)
        routed = -(-at // W2)
        tok = carve(XT, dt=U32)
        rec_at = carve(XT, dt=I32)
        top, top_i, pick = (carve(CB, TOP_PAD) for _ in range(3))
        scal = carve(6, CB)
        chosen = carve(2, CB)
        picked = carve(2, NE * CB)
        member, total, cumul, place = (carve(NE * CB) for _ in range(4))
        spot, lane_f, tile_f = (carve(2, CB) for _ in range(3))
        spot_i, part_i = (carve(2 * CB, dt=I32) for _ in range(2))
        ex = carve(8, NE)
        counts_i = carve(NE, dt=I32)
        tile_hot = carve(CB * CT).bitcast(F16)
        past = carve(CT, NE - 1)
        sorting = -(-at // W2)
        row_b3 = carve(NE * D)[0:1, :]
        record_clear = [-(-(at + (expert_i + 1) * REC) // W2) for expert_i in range(NE)]
        records = carve(NE, REC)
        records_flat = records.rearrange("p a b -> p (a b)")
        loaded = -(-at // W2)
        xT = carve(2, KD * P)
        h1, h2 = carve(KH * P), carve(KH * P)
        YB, YG, XR = 3, 6, 4
        y_out = carve(YB, D)
        y_in = carve(YG, D)
        assert at <= NB * W2
        XG = 4
        XD = 8
        wbuf = arena[:, 0:2 * W12].rearrange("p (r w) -> p r w", r=2)
        xg = arena[:, 2 * W12:2 * W12 + XR * D].rearrange("p (r d) -> p r d", r=XR)
        lane_hot = arena[:, (2 * XG + XD) * D:(2 * XG + XD) * D + CB * P // 2].bitcast(F16).rearrange("p (b m) -> p b m", b=CB)
        assert (2 * XG + XD) * D + CB * P // 2 <= SLOTS * W1 + 2 * D and 2 * W12 + XR * D <= (2 * XG + XD) * D

        xn_at, xn_out, turned2, moved2, rh_at, log_ps, log_at, xnT_read = ({} for _ in range(8))
        sorted_at, gate_at, ready = {}, {}, {}
        l_xn = [lane("l_xn0"), lane("l_xn1")]
        l_ew = lane("l_ew")
        l_rw = lane("l_rw")

        def load_router():
            clear = [x1_at[routed]]
            sp.dma(l_rw, r1, rw1.rearrange("(k p) n -> p k n", p=P), after=clear)
            sp.dma(l_rw, r2, rw2)
            sp.dma(l_rw, bias_rows[0:NE * KH, :], eb1.rearrange("e (k p) -> (e k) p", p=P))
            sp.dma(l_rw, bias_rows[NE * KH:2 * NE * KH, :], eb2.rearrange("e (k p) -> (e k) p", p=P))
            sp.dma(l_rw, bias_rows[2 * NE * KH:NBR, :], rb1.rearrange("(a n) -> a n", a=1))
            ready["rw"] = sp.dma(l_rw, row_b2, rb2.rearrange("(a n) -> a n", a=1))
            t = pe.put(lambda e: e.transpose(ps[5][:, 0:NBR], bias_rows, ident[0:NBR, 0:NBR]),
                       after=[ready["rw"], sums2])
            ready["bias"] = act.put(lambda e: e.activation(bias_cols, ps[5][:, 0:NBR], ACT.Copy), after=[t])
            ready["pad"] = dve.put(lambda e: e.memset(logits, -1e30), after=clear)
            ready["lane"] = pool.put(lambda e: e.iota(lane_no, [[0, 1]], base=0, channel_multiplier=1,
                                                       allow_small_or_imprecise_dtypes=True), after=clear)

        def load_expert(expert_i):
            if expert_i == 0:
                sp.dma(l_ew, row_b3, eb3.rearrange("(a e) n -> a (e n)", a=1), after=[x1_at[record_clear[0]]])
            for at_, a in ((0, ew1), (KD * HID, ew2), (W12, ew3)):
                ready["ew"] = sp.dma(l_ew, records[:, expert_i, at_:at_ + KH * D].rearrange("p (k n) -> p k n", k=KH),
                                     a[expert_i].rearrange("(k p) n -> p k n", p=P), after=[x1_at[record_clear[expert_i]]])

        def spread_biases():
            b3_at = {}
            clear = [x1_at[loaded]]
            assert loaded < NB - 5
            for i in range(2):
                a = act.put(lambda e, i=i: e.activation(
                    records[:, :, W12 - 2 * KH + i * KH:W12 - KH + i * KH],
                    bias_cols[:, i * NE * KH:(i + 1) * NE * KH].rearrange("p (e k) -> p e k", e=NE), ACT.Copy),
                    after=clear + [ready["bias"]])
            for expert_i in range(NE):
                t = pe.put(lambda e, expert_i=expert_i: e.matmul(ps[expert_i % 2][:, 0:D], ones[0:1, :],
                                                       row_b3[:, expert_i * D:(expert_i + 1) * D], start=True, stop=True),
                           after=[ready["ew"], sums2] + ([b3_at[expert_i - 2]] if expert_i >= 2 else []))
                b3_at[expert_i] = act.put(lambda e, expert_i=expert_i: e.activation(
                    records[:, expert_i, W12 + KH * D:REC], ps[expert_i % 2][:, 0:D], ACT.Copy), after=[t])
            ready["records"] = b3_at[NE - 1]

        scale_at = {}

        def route(g, done):
            blocks = groups[g]
            b0, n = blocks[0], len(blocks)
            if g not in scale_at:
                z = max(h for h in range(g, len(groups)) if groups[h][-1] <= done)
                span = groups[z][-1] + 1 - b0
                scale_at.update((h, None) for h in range(g, z + 1))
                for b in range(b0, b0 + span):
                    v = dve.put(lambda e, b=b: e.bn_aggr(mv[:, b, :], stats[:, b, :]), after=[stat[b]])
                rest = layer_norm_steps([v], b0, span)
                next(rest)
                yield
                v = next(rest)
                v = dve.put(lambda e: e.scalar_tensor_tensor(
                    shift[:, b0:b0 + span], mv[:, b0:b0 + span, 0], -1.0, rstd[:, b0:b0 + span], ALU.mult, ALU.mult),
                    after=[v])
                scale_at.update((h, v) for h in range(g, z + 1))
            else:
                yield
            for i, b in enumerate(blocks):
                xn_at[g] = act.put(lambda e, i=i, b=b: e.activation(
                    xn[g % 2][:, i, :], node[:, b, :], ACT.Identity, bias=shift[:, b:b + 1], scale=rstd[:, b:b + 1]),
                    after=[scale_at[g], x1_at[routed]] + ([turned2[g - 2], xn_out[g - 2]] if g >= 2 else []))
            yield
            xn_out[g] = sp.dma(l_xn[g % 2], xn_table[b0 * P:(b0 + n) * P, :].rearrange("(b p) d -> p b d", p=P),
                               xn[g % 2][:, 0:n, :], after=[xn_at[g], sums2])
            for j in range(0, n, 2):
                bank, m = ps[4], min(2, n - j)
                free = [moved] if j else [moved2[g - 1]] if g else [sums2]
                for i in range(m):
                    for k in range(KD):
                        at = (i * KD + k) * P
                        turned2[g] = pe.put(lambda e, i=i, j=j, k=k, at=at, bank=bank: e.transpose(
                            bank[:, at:at + P], xn[g % 2][:, j + i, k * P:(k + 1) * P], ident[:, :]),
                            after=[xn_at[g]] + free)
                moved = act.put(lambda e, j=j, m=m, bank=bank: e.activation(
                    xnT[g % 2][:, j:j + m, :, :].rearrange("p b k m -> p (b k m)"), bank[:, 0:m * D], ACT.Copy),
                    after=[turned2[g]] + ([xnT_read[g - 2]] if g >= 2 else []))
            moved2[g] = moved
            yield
            for k in range(KD):
                t = pe.put(lambda e, k=k: e.matmul(ps[5][:, 0:n * P], r1[:, k, :], xnT[g % 2][:, 0:n, k, :],
                                                   start=(k == 0), stop=(k == KD - 1)),
                           after=[moved2[g], ready["bias"]] + ([rh_at[g - 1]] if g else []))
            xnT_read[g] = t
            rh_at[g] = act.put(lambda e: e.activation(rh[:, 0:n * P], ps[5][:, 0:n * P], ACT.Relu, bias=br1),
                               after=[t] + ([log_ps[g - 1]] if g else []))
            yield
            for i in range(n):
                pe.put(lambda e, i=i: e.matmul(ps[6][:, i * TOP_PAD:i * TOP_PAD + NE], rh[:, i * P:(i + 1) * P], r2,
                                               start=True, stop=False),
                       after=[rh_at[g]] + ([log_at[g - 1]] if g else []))
                log_ps[g] = pe.put(lambda e, i=i: e.matmul(ps[6][:, i * TOP_PAD:i * TOP_PAD + NE], ones[0:1, :],
                                                           row_b2, start=False, stop=True))
            yield
            log_at[g] = dve.put(lambda e: e.tensor_copy(
                logits[:, b0:b0 + n, 0:NE],
                ps[6][:, 0:n * TOP_PAD].rearrange("p (i m) -> p i m", m=TOP_PAD)[:, :, 0:NE]),
                after=[log_ps[g], ready["pad"]])

        def sort_chunk(s):
            blocks, nt = chunks[s], tiles_in[s]
            b0, n = blocks[0], len(blocks)
            lg = logits[:, b0:b0 + n, :]
            shape = [P, n, TOP_PAD]
            top_u = top_i.bitcast(U32)
            pk = pick[:, 0:n, :]
            s_sum, s_p1, s_p2, s_w1, s_w2, s_d = (scal[:, i, 0:n] for i in range(6))
            v = log_at[blocks[-1] // GROUP]
            was = [sorted_at[s - 1]] if s else [x1_at[sorting]]
            for i in range(n):
                v_t = dve.put(lambda e, i=i: e.max(top[:, i, :], lg[:, i, :]), after=[v] + was)
            yield
            for i in range(n):
                v_t = dve.put(lambda e, i=i: e.max_index(top_u[:, i, :], top[:, i, :], lg[:, i, :]), after=[v_t])
            yield
            v = dve.put(lambda e: e.tensor_tensor(pk, lg, top[:, 0:n, 0:1].to_broadcast(shape), ALU.subtract),
                        after=[v_t])
            a = act.put(lambda e: e.activation(pk, pk, ACT.Exp), after=[v])
            v = dve.put(lambda e: e.tensor_tensor(s_d, top[:, 0:n, 1], top[:, 0:n, 0], ALU.subtract), after=[v_t])
            a2 = act.put(lambda e: e.activation(s_p2, s_d, ACT.Exp), after=[v])
            yield
            v = dve.put(lambda e: e.tensor_reduce(s_sum, pk[:, :, 0:NE], AX_X, ALU.add), after=[a])
            v = dve.put(lambda e: e.reciprocal(s_p1, s_sum), after=[v])
            v = dve.put(lambda e: e.tensor_tensor(s_p2, s_p2, s_p1, ALU.mult), after=[a2, v])
            v = dve.put(lambda e: e.tensor_tensor(s_d, s_p2, s_p1, ALU.subtract), after=[v])
            a = act.put(lambda e: e.activation(s_w2, s_d, ACT.Exp), after=[v])
            v = dve.put(lambda e: e.tensor_copy(chosen[:, :, 0:n], top_u[:, 0:n, 0:2].rearrange("p b c -> p c b")),
                        after=[v_t])
            by_expert = [P, NE, n]
            is_ = [picked[:, c, 0:NE * n].rearrange("p (a b) -> p a b", a=NE) for c in range(2)]
            mem, tot, cum, plc = (t[:, 0:NE * n].rearrange("p (a b) -> p a b", a=NE)
                                  for t in (member, total, cumul, place))
            for c in range(2):
                v_is = dve.put(lambda e, c=c: e.tensor_tensor(
                    is_[c], iota[:, 0:NE].unsqueeze(2).to_broadcast(by_expert),
                    chosen[:, c, 0:n].unsqueeze(1).to_broadcast(by_expert), ALU.is_equal), after=[v])
            v_m = dve.put(lambda e: e.tensor_tensor(mem, is_[0], is_[1], ALU.add), after=[v_is])
            t_b = pe.put(lambda e: e.matmul(ps[7][:, 0:NE * n], below[:, :], member[:, 0:NE * n],
                                            start=True, stop=True), after=[v_m, sums2] + was)
            t_a = pe.put(lambda e: e.matmul(ps[7][:, 256:256 + NE * n], ones[:, :], member[:, 0:NE * n],
                                            start=True, stop=True))
            yield
            v = dve.put(lambda e: e.tensor_scalar(s_w1, s_w2, 1.0, None, ALU.add), after=[a])
            v = dve.put(lambda e: e.reciprocal(gate[:, 0, b0:b0 + n], s_w1), after=[v])
            gate_at[s] = dve.put(lambda e: e.tensor_tensor(gate[:, 1, b0:b0 + n], s_w2, gate[:, 0, b0:b0 + n],
                                                           ALU.mult), after=[v])
            v = dve.put(lambda e: e.tensor_copy(total[:, 0:NE * n], ps[7][:, 256:256 + NE * n]), after=[t_a])
            v = dve.put(lambda e: e.tensor_tensor_scan(cumul[:, 0:NE * n], total[:, 0:NE * n], total[:, 0:NE * n],
                                                       0.0, ALU.add, ALU.bypass), after=[v])
            prev, own, tiles, upto_t, first_t, off = (ex[:, i, :] for i in range(6))
            yield
            v = dve.put(lambda e: e.memset(prev[:, 0:1], 0.0), after=[v])
            v = dve.put(lambda e: e.tensor_copy(prev[:, 1:NE], cum[:, 0:NE - 1, n - 1]), after=[v])
            v = dve.put(lambda e: e.tensor_tensor(own, cum[:, :, n - 1], prev, ALU.subtract), after=[v])
            v = dve.put(lambda e: e.tensor_scalar(counts_i, own, float(P - 1), None, ALU.add), after=[v])
            v = dve.put(lambda e: e.tensor_scalar(counts_i, counts_i, 7, None, ALU.logical_shift_right), after=[v])
            v = dve.put(lambda e: e.tensor_copy(tiles, counts_i), after=[v])
            v = dve.put(lambda e: e.tensor_tensor_scan(upto_t, tiles, tiles, 0.0, ALU.add, ALU.bypass), after=[v])
            v = dve.put(lambda e: e.tensor_tensor(first_t, upto_t, tiles, ALU.subtract), after=[v])
            v = dve.put(lambda e: e.scalar_tensor_tensor(off, first_t, float(P), prev, ALU.mult, ALU.subtract),
                        after=[v])
            yield
            v = dve.put(lambda e: e.tensor_tensor(plc, cum, tot, ALU.subtract), after=[v])
            v = dve.put(lambda e: e.tensor_tensor(plc, plc, off.unsqueeze(2).to_broadcast(by_expert), ALU.add),
                        after=[v])
            v = dve.put(lambda e: e.tensor_tensor(place[:, 0:NE * n], place[:, 0:NE * n], ps[7][:, 0:NE * n],
                                                  ALU.add), after=[v, t_b])
            for c in range(2):
                v_p = dve.put(lambda e, c=c: e.tensor_tensor(is_[c], is_[c], plc, ALU.mult), after=[v])
            for c in range(2):
                v = dve.put(lambda e, c=c: e.tensor_reduce(spot[:, c, 0:n], is_[c].rearrange("p a b -> p b a"),
                                                           AX_X, ALU.add), after=[v_p])
            spots = spot_i.rearrange("p (c b) -> p c b", c=2)[:, :, 0:n]
            parts = part_i.rearrange("p (c b) -> p c b", c=2)[:, :, 0:n]
            v = dve.put(lambda e: e.tensor_copy(y_row[:, :, b0:b0 + n], spot[:, :, 0:n]), after=[v])
            yield
            v = dve.put(lambda e: e.tensor_copy(spots, spot[:, :, 0:n]), after=[v])
            v = dve.put(lambda e: e.tensor_scalar(parts, spots, P - 1, None, ALU.bitwise_and), after=[v])
            v = dve.put(lambda e: e.tensor_copy(lane_f[:, :, 0:n], parts), after=[v])
            v = dve.put(lambda e: e.tensor_scalar(parts, spots, 7, None, ALU.logical_shift_right), after=[v])
            v = dve.put(lambda e: e.tensor_copy(tile_f[:, :, 0:n], parts), after=[v])
            v = dve.put(lambda e: e.tensor_tensor(
                past[:, 0:nt, :], iota[:, 0:nt].unsqueeze(2).to_broadcast([P, nt, NE - 1]),
                upto_t[:, 0:NE - 1].unsqueeze(1).to_broadcast([P, nt, NE - 1]), ALU.is_ge), after=[v])
            v = dve.put(lambda e: e.tensor_reduce(cumul[:, 0:nt], past[:, 0:nt, :], AX_X, ALU.add), after=[v])
            v = ready["rec", s] = dve.put(lambda e: e.tensor_scalar(
                rec_at[:, tile0[s]:tile0[s] + nt], cumul[:, 0:nt], float(REC), None, ALU.mult), after=[v])
            assert NB <= 2048 and NE * CB <= 256
            th = tile_hot[:, 0:2 * n * nt].rearrange("p (a b j) -> p a b j", a=2, b=n)
            wide = [P, n, nt]
            hot_read = []
            for c in range(2):
                yield
                v = dve.put(lambda e, c=c: e.tensor_tensor(
                    th[:, 1, :, :], iota[:, 0:nt].unsqueeze(1).to_broadcast(wide),
                    tile_f[:, c, 0:n].unsqueeze(2).to_broadcast(wide), ALU.is_equal), after=[v] + hot_read)
                v = dve.put(lambda e: e.tensor_scalar(th[:, 0, :, :], th[:, 1, :, :], lane_no, None, ALU.mult),
                            after=[v, ready["lane"]])
                v = dve.put(lambda e: e.tensor_tensor(
                    th[:, 1, :, :], th[:, 1, :, :], iota[:, b0:b0 + n].unsqueeze(2).to_broadcast(wide), ALU.mult),
                    after=[v])
                yield
                v = dve.put(lambda e, c=c: e.tensor_tensor(
                    lane_hot[:, 0:n, :], iota[:, :].unsqueeze(1).to_broadcast([P, n, P]),
                    lane_f[:, c, 0:n].unsqueeze(2).to_broadcast([P, n, P]), ALU.is_equal), after=[v, sums2])
                for i in range(n):
                    t = pe.put(lambda e, c=c, i=i: e.matmul(
                        ps[7][:, 0:2 * nt].rearrange("p (a j) -> p a j", a=2), lane_hot[:, i, :], th[:, :, i, :],
                        start=(c == 0 and i == 0), stop=(c == 1 and i == n - 1)), after=[v])
                hot_read = [t]
            yield
            v = dve.put(lambda e: e.tensor_copy(cumul[:, 0:nt], ps[7][:, 0:nt]), after=[t])
            sorted_at[s] = dve.put(lambda e: e.scalar_tensor_tensor(
                tok[:, tile0[s]:tile0[s] + nt], ps[7][:, nt:2 * nt], float(P), cumul[:, 0:nt], ALU.mult, ALU.add),
                after=[v])

        sq = acc.rearrange("p (b w) -> p b w", w=W2)
        l_xr = [lane("l_xr0"), lane("l_xr1")]
        xr = arena[:, 0:2 * XG * D].rearrange("p (h r d) -> p h r d", h=2, r=XG)
        mid = arena[:, 2 * XG * D:2 * XG * D + XD * D].rearrange("p (r d) -> p r d", d=D)
        x1_at, tanh_at, prod_at, got_xr, stat = {}, {}, {}, {}, {}
        v_half = dve.put(lambda e: e.tensor_scalar(deg[:, :], deg[:, :], 0.5, None, ALU.mult), after=[sums2, v_rden])

        def reload_x(g):
            b, nb = g * XG, min(XG, NB - g * XG)
            full = min(nb, NB - 1 - b)
            free = [x1_at[b - XG - 1]] if g >= 2 else [sums2]
            if full:
                got_xr[g] = sp.dma(l_xr[g % 2], xr[:, g % 2, 0:full, :],
                                   x[b * P:(b + full) * P, :].rearrange("(b p) d -> p b d", p=P), after=free)
            if full < nb:
                zr = pool.put(lambda e: e.memset(xr[:, g % 2, full, :], 0.0), after=free)
                got_xr[g] = sp.dma(l_xr[g % 2], xr[0:LAST, g % 2, full, :], x[(NB - 1) * P:N, :], after=[zr])

        def half_products(b):
            t1 = mid[:, b % XD, :]
            v = dve.put(lambda e: e.scalar_tensor_tensor(t1, node[:, b, :], deg[:, b:b + 1], sq[:, b, 0:D],
                                                         ALU.mult, ALU.subtract),
                        after=[v_half, h_at[NB - 1]] + ([x1_at[b - XD]] if b >= XD else []))
            prod_at[b] = pool.put(lambda e: e.tensor_tensor(t1, t1, node[:, b, :], ALU.mult), after=[v])

        def finish_x1(b):
            t1 = mid[:, b % XD, :]
            v = dve.put(lambda e: e.scalar_tensor_tensor(t1, t1, 2.0, sq[:, b, D:W2], ALU.mult, ALU.add),
                        after=[prod_at[b]])
            tanh_at[b] = act.put(lambda e: e.activation(t1, t1, ACT.Tanh, scale=rden[:, b:b + 1]), after=[v])

        def add_x(b):
            g, i = divmod(b, XG)
            x1_at[b] = pool.put(lambda e: e.tensor_tensor(node[:, b, :], mid[:, b % XD, :], xr[:, g % 2, i, :],
                                                          ALU.add), after=[tanh_at[b], got_xr[g], prod_at[b]])

        def stats_x1(b):
            stat[b] = dve.put(lambda e: e.bn_stats(stats[:, b, :], node[:, b, :]), after=[x1_at[b]])

        routing, sorting_now, started, asked = [], [], 0, False

        def behind(done):
            nonlocal started, asked
            if done >= routed and not asked:
                load_router()
                asked = True
            if sorting_now and next(sorting_now[0], "end") == "end":
                sorting_now.pop(0)
            if done % 2 == 0 and done < NB - 1:
                return
            under_way = list(routing)
            if asked and started < len(groups) and groups[started][-1] <= done:
                routing.append(route(started, done))
                next(routing[-1])
                started += 1
            for r in under_way:
                if next(r, "end") == "end":
                    routing.remove(r)
                    if started - len(routing) in cut[1:]:
                        sorting_now.append(sort_chunk(cut.index(started - len(routing)) - 1))

        reload_x(0)
        reload_x(1)
        SKEW = 2
        for i in range(NB + 3 * SKEW):
            b = i - 2 * SKEW
            if 0 <= b < NB:
                add_x(b)
                if b % XG == XG - 1 and (b // XG + 2) * XG < NB:
                    reload_x(b // XG + 2)
                if b == NB - 5:
                    spread_biases()
                if b in record_clear:
                    load_expert(record_clear.index(b))
            if i < NB:
                half_products(i)
            if 0 <= i - SKEW < NB:
                finish_x1(i - SKEW)
            if i >= 3 * SKEW:
                stats_x1(i - 3 * SKEW)
                behind(i - 3 * SKEW)
        while 0 not in sorted_at:
            behind(NB - 1)

        done1 = x1_at[NB - 1]
        y_table = [nc.dram_tensor(f"y_table{s}", [c * P, D], F32, kind="Internal").ap() for s, c in enumerate(tiles_in)]
        l_x = [lane(f"l_x{i}") for i in range(XR)]
        l_y = [lane(f"l_y{i}") for i in range(YB)]
        l_back = [lane(f"l_back{i}") for i in range(YG)]
        l_out = lane("l_out")
        got_x1, turned, moved, copied, t1_at, h1_at, t2_at, h2_at, t3_at, y_at, y_sent = ({} for _ in range(11))
        dve_rec, pe_rec = {}, {}
        chunk_of = [s for s, c in enumerate(tiles_in) for _ in range(c)]

        def record_of(k, engine, kept):
            def issue(e):
                kept[k] = nc.values_load(rec_at[0:1, k:k + 1], engines=[engine], min_val=0, max_val=(NE - 1) * REC,
                                         skip_runtime_bounds_check_because="a tile's expert is below NE")
            return issue

        def fetch(k):
            s = chunk_of[k]
            last = chunks[s][-1] // GROUP
            got_x1[k] = pool.put(lambda e: e.indirect_dma_start(
                out=xg[:, k % XR, :], out_offset=None, in_=xn_table,
                in_offset=bass.IndirectOffsetOnAxis(ap=tok[:, k:k + 1], axis=0)),
                after=[sorted_at[s], xn_out[last], xn_out[last - 1], done1] + ([turned[k - XR]] if k >= XR else []),
                lane=l_x[k % XR], by=16)

        def turn(k):
            for j in range(KD):
                turned[k] = pe.put(lambda e, j=j: e.transpose(
                    ps[0][:, j * P:(j + 1) * P], xg[:, k % XR, j * P:(j + 1) * P], ident[:, :]),
                    after=[got_x1[k]] + ([moved[k - 1]] if k else [ready["records"]]))
            moved[k] = act.put(lambda e: e.activation(xT[:, k % 2, :], ps[0][:, 0:D], ACT.Copy),
                               after=[turned[k], done1] + ([t1_at[k - 2]] if k >= 2 else []))

        def weights(k):
            dve.prepare(record_of(k, mybir.EngineType.DVE, dve_rec), after=[ready["rec", chunk_of[k]]])
            copied[k] = dve.put(lambda e: e.tensor_copy(wbuf[:, k % 2, :], records_flat[:, bass.ds(dve_rec[k], W12)]),
                                after=[ready["records"], done1] + ([h2_at[k - 2]] if k >= 2 else []))

        def layer(k, bank, left_at, moving, free, out_h, out_free, bias_at):
            for m in range(KH):
                for j in range(KD):
                    left = left_at + j * HID + m * P
                    t = pe.put(lambda e, m=m, j=j, left=left: e.matmul(
                        ps[bank][:, m * P:(m + 1) * P], wbuf[:, k % 2, left:left + P], moving[:, j * P:(j + 1) * P],
                        start=(j == 0), stop=(j == KD - 1)), after=free)
            for m in range(KH):
                a = act.put(lambda e, m=m: e.activation(
                    out_h[:, m * P:(m + 1) * P], ps[bank][:, m * P:(m + 1) * P], ACT.Relu,
                    bias=wbuf[:, k % 2, bias_at + m:bias_at + m + 1]), after=[t] + out_free)
            return t, a

        def layer1(k):
            t1_at[k], h1_at[k] = layer(
                k, 1, 0, xT[:, k % 2, :], [moved[k], copied[k]] + ([h1_at[k - 1]] if k else []),
                h1, [t2_at[k - 1]] if k else [done1], W12 - 2 * KH)

        def layer2(k):
            t2_at[k], h2_at[k] = layer(
                k, 2, KD * HID, h1, [h1_at[k]] + ([h2_at[k - 1]] if k else []),
                h2, [t3_at[k - 1]] if k else [done1], W12 - KH)

        def layer3(k):
            pe.prepare(record_of(k, mybir.EngineType.PE, pe_rec), after=[ready["rec", chunk_of[k]]])
            for j in range(KH):
                t3_at[k] = pe.put(lambda e, j=j: e.matmul(
                    ps[3][:, 0:D], h2[:, j * P:(j + 1) * P],
                    records_flat[:, bass.ds(pe_rec[k] + (W12 + j * D), D)], start=(j == 0), stop=(j == KH - 1)),
                    after=[h2_at[k], ready["records"]] + ([y_at[k - 1]] if k else []))

        def finish(k):
            y_at[k] = dve.put(lambda e: e.tensor_tensor(
                y_out[:, k % YB, :], ps[3][:, 0:D], records_flat[:, bass.ds(dve_rec[k] + (W12 + KH * D), D)],
                ALU.add), after=[t3_at[k], done1] + ([y_sent[k - YB]] if k >= YB else []))
            s = chunk_of[k]
            row = (k - tile0[s]) * P
            y_sent[k] = sp.dma(l_y[k % YB], y_table[s][row:row + P, :], y_out[:, k % YB, :], after=[y_at[k]])

        back, added = {}, {}

        def bring_back(b):
            s = [b in c for c in chunks].index(True)
            for c in range(2):
                i = 2 * b + c
                back[i] = pool.put(lambda e, c=c, i=i: e.indirect_dma_start(
                    out=y_in[:, i % YG, :], out_offset=None, in_=y_table[s],
                    in_offset=bass.IndirectOffsetOnAxis(ap=y_row[:, c, b:b + 1], axis=0)),
                    after=[y_sent[tile0[s + 1] - 1 - j] for j in range(YB)] + [done1]
                    + ([added[i - YG]] if i >= YG else []), lane=l_back[i % YG], by=16)

        def add_back(b):
            nonlocal stored
            for c in range(2):
                i = 2 * b + c
                added[i] = dve.put(lambda e, c=c, i=i: e.scalar_tensor_tensor(
                    node[:, b, :], y_in[:, i % YG, :], gate[:, c, b:b + 1], node[:, b, :], ALU.mult, ALU.add),
                    after=[back[i]] + ([added[i - 1]] if c else []))
            g = b // GROUP
            if b == groups[g][-1]:
                b0 = groups[g][0]
                full = b + 1 if b < NB - 1 else b
                if full > b0:
                    stored = sp.dma(l_out, out[b0 * P:full * P, :].rearrange("(b p) d -> p b d", p=P),
                                    node[:, b0:full, :], after=[added[i]])
                if b == NB - 1:
                    stored = sp.dma(l_out, out[b * P:N, :], node[0:LAST, b, :], after=[added[i]])

        stored = None
        AHEAD = 4
        for k in range(AHEAD):
            fetch(k)
        for k in range(2):
            turn(k)
            weights(k)
        layer1(0)
        for k in range(XT):
            s = chunk_of[k]
            j = k - tile0[s]
            if k + 2 < XT:
                turn(k + 2)
            layer2(k)
            if k + 1 < XT:
                layer1(k + 1)
            if k:
                finish(k - 1)
            if k + 2 < XT:
                weights(k + 2)
            layer3(k)
            if sorting_now or routing or started < len(groups):
                behind(NB - 1)
            if k + AHEAD < XT:
                fetch(k + AHEAD)
            if s:
                before_ = chunks[s - 1]
                space = (tiles_in[s] - 4) / len(before_)
                for i, b in enumerate(before_):
                    at_ = 4 + int(i * space)
                    if j == at_:
                        bring_back(b)
                    if j == min(at_ + 2, tiles_in[s] - 1):
                        add_back(b)
        finish(XT - 1)
        for i, b in enumerate(chunks[-1]):
            bring_back(b)
            if i >= 1:
                add_back(b - 1)
        add_back(NB - 1)
        for done in (stored, h_written, seg_out, list_zeroed, scattered, *xn_out.values(), *y_sent.values()):
            sp.wait(done)

        block = ctx.enter_context(nc.Block())

        @block.sync
        def _(e):
            sp.run(e)

        @block.tensor
        def _(e):
            pe.run(e)

        @block.vector
        def _(e):
            dve.run(e)

        @block.scalar
        def _(e):
            act.run(e)

        @block.gpsimd
        def _(e):
            pool.run(e)


_INS = ["x", "src", "dst", "L0_gnn_W_root", "L0_gnn_W_neigh", "L0_gnn_b", "L0_ffn_router_w1", "L0_ffn_router_b1",
        "L0_ffn_router_w2", "L0_ffn_router_b2", "L0_ffn_expert_w1", "L0_ffn_expert_b1", "L0_ffn_expert_w2",
        "L0_ffn_expert_b2", "L0_ffn_expert_w3", "L0_ffn_expert_b3"]


def kernel(**inputs):
    import numpy as np
    import concourse.bacc as bacc
    from concourse.bass_utils import run_bass_kernel_spmd

    nc = bacc.Bacc("TRN2", target_bir_lowering=False, num_devices=1)
    arrays, args = {}, []
    for name in _INS:
        a = np.ascontiguousarray(inputs[name])
        arrays[f"in_{name}"] = a
        args.append(nc.dram_tensor(f"in_{name}", a.shape, mybir.dt.from_np(a.dtype), kind="ExternalInput").ap())
    args.append(nc.dram_tensor("result", arrays["in_x"].shape, F32, kind="ExternalOutput").ap())
    gnn_moe_kernel(nc, *args)
    done = run_bass_kernel_spmd(nc, [arrays], core_ids=[0])
    return done.results[0]["result"]
```
